# Optimizing a Trainium2 kernel written in Bass

```python
import numpy as np
import jax
import jax.numpy as jnp

def _softmax(x, axis=-1):
    return jax.nn.softmax(x, axis=axis)

def _gelu(x):
    return jax.nn.gelu(x, approximate=True)

def _silu(x):
    return jax.nn.silu(x)

def _sigmoid(x):
    return jax.nn.sigmoid(x)

def _layernorm(x, axis=-1, eps=1e-05):
    m = jnp.mean(x, axis=axis, keepdims=True)
    v = jnp.var(x, axis=axis, keepdims=True)
    return (x - m) / jnp.sqrt(v + eps)

def _scatter_add(tgt, idx, src, axis=0):
    return tgt.at[idx].add(src)

def _segment_sum(src, seg, n):
    return jax.ops.segment_sum(src, seg, n)
kernel_name = 'mk_adj_preln_d1_adj_r2_0d8357'

def setup_inputs(seed: int=0):
    np.random.seed(seed)
    _w = jnp.asarray

    def _rec_inputs():
        import jax
        import jax.numpy as jnp
        _gk = jax.random.key(seed)
        x = -0.0002928 + 1 * jax.random.normal(jax.random.fold_in(_gk, 1), (1354, 512), jnp.float32)
        _w = (1.0 + jnp.arange(1354, dtype=jnp.float32)) ** (-0.5)
        _w = _w / _w.mean()
        _pij = jnp.clip(0.0118168 * _w[:, None] * _w[None, :], 0.0, 1.0)
        _a = jax.random.uniform(jax.random.fold_in(_gk, 2), (1354, 1354)) < _pij
        _a = jnp.logical_or(_a, jnp.eye(1354, dtype=bool))
        _af = _a.astype(jnp.float32)
        _af = _af * jax.random.uniform(jax.random.fold_in(_gk, 3), (1354, 1354), jnp.float32, 0.05, 1)
        adj = _af
        return (x, adj)
    x, adj = _rec_inputs()

    def _L0_gnn_setup():
        import jax, jax.numpy as jnp
        import numpy as np
        D_IN, D_ATTN, STEPS = (512, 64, 2)
        P_TOP, TAU, LN_EPS = (0.9, 1.0, 1e-05)
        N = 2048

        def _xavier(key, shape):
            fan_in, fan_out = (shape[0], shape[1])
            lim = jnp.sqrt(6.0 / (fan_in + fan_out))
            return jax.random.uniform(key, shape, jnp.float32, -lim, lim)

        def _adj_from_feats(Xa, W1, W2, W3):
            Q = Xa @ W1
            K = Xa @ W3
            logits = Q @ W2 @ K.T / TAU
            n = logits.shape[1]
            order = jnp.argsort(-logits, axis=1)
            vals = jnp.take_along_axis(logits, order, axis=1)
            probs = jax.nn.softmax(vals, axis=1)
            csum = jnp.cumsum(probs, axis=1)
            k_i = jnp.sum(csum < P_TOP, axis=1) + 1
            keep = jnp.arange(n)[None, :] < k_i[:, None]
            masked_sorted = jnp.where(keep, vals, -jnp.inf)
            rows = jnp.arange(n)[:, None]
            masked = jnp.full_like(logits, -jnp.inf).at[rows, order].set(masked_sorted)
            return jax.nn.softmax(masked, axis=1)
        key = jax.random.key(seed)
        ks = jax.random.split(key, 12)
        X = jax.random.normal(ks[0], (N, D_IN), jnp.float32)
        S = jax.random.uniform(ks[1], (N, N), jnp.float32)
        W1 = _xavier(ks[2], (D_IN, D_ATTN))
        W3 = _xavier(ks[3], (D_IN, D_ATTN))
        W2 = _xavier(ks[4], (D_ATTN, D_ATTN))
        U1_0 = _xavier(ks[5], (D_IN, D_IN))
        U1_1 = _xavier(ks[6], (D_IN, D_IN))
        U2_0 = _xavier(ks[7], (D_IN, D_IN))
        U2_1 = _xavier(ks[8], (D_IN, D_IN))
        gamma = jnp.ones((D_IN,), jnp.float32)
        beta = jnp.zeros((D_IN,), jnp.float32)
        return {'X': X, 'S': S, 'W1': W1, 'W2': W2, 'W3': W3, 'U1_0': U1_0, 'U1_1': U1_1, 'U2_0': U2_0, 'U2_1': U2_1, 'gamma': gamma, 'beta': beta}
    _L0_gnn_all = _L0_gnn_setup()
    _L0_gnn_in = {k: v for k, v in _L0_gnn_all.items() if k in ('W1', 'W2', 'W3', 'U1_0', 'U1_1', 'U2_0', 'U2_1', 'gamma', 'beta')}
    del _L0_gnn_all
    return {'x': x, 'adj': adj, 'L0_gnn_W1': _L0_gnn_in['W1'], 'L0_gnn_W2': _L0_gnn_in['W2'], 'L0_gnn_W3': _L0_gnn_in['W3'], 'L0_gnn_U1_0': _L0_gnn_in['U1_0'], 'L0_gnn_U1_1': _L0_gnn_in['U1_1'], 'L0_gnn_U2_0': _L0_gnn_in['U2_0'], 'L0_gnn_U2_1': _L0_gnn_in['U2_1'], 'L0_gnn_gamma': _L0_gnn_in['gamma'], 'L0_gnn_beta': _L0_gnn_in['beta']}

def reference(x, adj, L0_gnn_W1, L0_gnn_W2, L0_gnn_W3, L0_gnn_U1_0, L0_gnn_U1_1, L0_gnn_U2_0, L0_gnn_U2_1, L0_gnn_gamma, L0_gnn_beta):
    import jax
    import jax.numpy as jnp

    def _L0_gnn_ref(X, S, W1, W2, W3, U1_0, U1_1, U2_0, U2_1, gamma, beta):
        import jax, jax.numpy as jnp
        import numpy as np
        D_IN, D_ATTN, STEPS = (512, 64, 2)
        P_TOP, TAU, LN_EPS = (0.9, 1.0, 1e-05)
        N = 2048

        def _xavier(key, shape):
            fan_in, fan_out = (shape[0], shape[1])
            lim = jnp.sqrt(6.0 / (fan_in + fan_out))
            return jax.random.uniform(key, shape, jnp.float32, -lim, lim)

        def _adj_from_feats(Xa, W1, W2, W3):
            Q = Xa @ W1
            K = Xa @ W3
            logits = Q @ W2 @ K.T / TAU
            n = logits.shape[1]
            order = jnp.argsort(-logits, axis=1)
            vals = jnp.take_along_axis(logits, order, axis=1)
            probs = jax.nn.softmax(vals, axis=1)
            csum = jnp.cumsum(probs, axis=1)
            k_i = jnp.sum(csum < P_TOP, axis=1) + 1
            keep = jnp.arange(n)[None, :] < k_i[:, None]
            masked_sorted = jnp.where(keep, vals, -jnp.inf)
            rows = jnp.arange(n)[:, None]
            masked = jnp.full_like(logits, -jnp.inf).at[rows, order].set(masked_sorted)
            return jax.nn.softmax(masked, axis=1)
        n = X.shape[0]
        S = S + jnp.eye(n, dtype=X.dtype)
        R = S / jnp.clip(S.sum(axis=1, keepdims=True), 1e-12)
        Z = jnp.zeros_like(X)
        Xf, Xa = (X, X)
        U1s, U2s = ((U1_0, U1_1), (U2_0, U2_1))
        for s in range(STEPS):
            A = _adj_from_feats(Xa, W1, W2, W3)
            Xf = R @ Xf
            Xa = A @ Xa
            Z = Z + (Xf @ U1s[s] + Xa @ U2s[s])
        Y = X + Z
        mu = Y.mean(axis=-1, keepdims=True)
        var = Y.var(axis=-1, keepdims=True)
        return (Y - mu) * jax.lax.rsqrt(var + LN_EPS) * gamma + beta
    h = jnp.maximum(_layernorm(x, axis=-1), 0.0)
    x = x + _L0_gnn_ref(h, adj, L0_gnn_W1, L0_gnn_W2, L0_gnn_W3, L0_gnn_U1_0, L0_gnn_U1_1, L0_gnn_U2_0, L0_gnn_U2_1, L0_gnn_gamma, L0_gnn_beta)
    return x

_drawn_inputs = setup_inputs


def setup_inputs(seed=0):
    import zlib

    import numpy as np

    out = dict(_drawn_inputs(seed))
    spreads = {'L0_gnn_gamma': (1.0, 0.2), 'L0_gnn_beta': (0.0, 0.1)}
    factors = {}
    for name, (base, spread) in spreads.items():
        noise = np.random.default_rng([zlib.crc32(name.encode()), seed]).standard_normal(out[name].shape)
        drawn = base * np.exp(spread * noise) if base else spread * noise
        out[name] = jnp.asarray(drawn.astype(out[name].dtype))
    for name, factor in factors.items():
        out[name] = (out[name] * factor).astype(out[name].dtype)
    return out
```

```python
import concourse.bass as bass
from concourse import mybir
from contextlib import ExitStack

FP32 = mybir.dt.float32
FP16 = mybir.dt.float16
INT32 = mybir.dt.int32
ALU = mybir.AluOpType
ACT = mybir.ActivationFunctionType
AX = mybir.AxisListType

N, D, DA, P = 1354, 512, 64, 128
NT = -(-N // P)
DC = D // P
LN_EPS, P_TOP = 1e-5, 0.9
STEPS = 2
SLOTS = 4
GROUPS = [list(range(a, min(a + SLOTS, NT))) for a in range(0, NT, SLOTS)]
CHUNKS = [(c, min(512, N - c)) for c in range(0, N, 512)]
BLOCKS = [list(range(a, min(a + 4, NT))) for a in range(0, NT, 4)]

SC_X = 256.0
SC_U = 1024.0
SC_S = 128.0
SC_P = 4096.0
SC_K = 256.0

EVALS = [4, 6]
WINDOWS = [1, 2]
GUESS = (2.65, -2.76, 0.2)
HI0 = 1.5
LOG_BITS = 0.6931472 / 2 ** 23
LOG_ONE = 126.95 * 0.6931472
RSQRT_BITS = float(0x5F3759DF)
ROUND_INT = 12582912.0


def rows(t):
    return min(P, N - t * P)


def schedule():
    yield ("prep",)
    for s in range(STEPS):
        for c in range(len(CHUNKS)):
            yield ("qk", s, c)
        for c in range(len(CHUNKS)):
            yield ("q2", s, c)
        for t in GROUPS[0]:
            yield ("logits", s, t)
        yield ("select", s, 0)
        side = ["into", "first"] if s == 0 else ["carry", "base"]
        for kind in side:
            for t in range(NT):
                yield (kind, t)
        if s == 0:
            yield ("rowsum",)
        for g, group in enumerate(GROUPS):
            if s == 1:
                for t in group:
                    yield ("spread", s, t)
            for i, t in enumerate(group):
                yield ("cut", s, t)
                if t + SLOTS < NT:
                    yield ("logits", s, t + SLOTS)
                if t > 0:
                    yield ("attend", s, t - 1)
                if t > 1 and s == 0:
                    yield ("turn", t - 2)
                if s == 1 and t > 1:
                    yield ("norm", t - 2)
            if g + 1 < len(GROUPS):
                yield ("select", s, g + 1)
            if s == 0:
                for t in group:
                    yield ("spread", s, t)
                if g == 0:
                    yield ("weights", 2)
        yield ("attend", s, NT - 1)
        for t in (NT - 2, NT - 1):
            yield ("turn", t) if s == 0 else ("norm", t)
        if s == 0:
            yield ("weights", 3)


ORDER = list(schedule())
BANK_READERS = {"qk": "av", "into": "a", "first": "a", "rowsum": "a", "spread": "a", "attend": "a", "carry": "a", "base": "a"}
TURN_READERS = {"ht": "av", "q2": "av", "cut": "a", "turn": "a"}


def bank_jobs():
    jobs = [o for o in ORDER if o[0] in BANK_READERS]
    return {o: n for n, o in enumerate(jobs)}, ["v" if o[:2] == ("attend", 1) else BANK_READERS[o[0]] for o in jobs]


def turn_jobs():
    jobs = [("ht", t) for t in range(NT)]
    for o in ORDER:
        if o[0] == "cut":
            jobs += [o + (b,) for b in range(len(BLOCKS))]
        elif o[0] in ("q2", "turn"):
            jobs.append(o)
    return {o: n for n, o in enumerate(jobs)}, [TURN_READERS[o[0]] for o in jobs]


BANK, BANK_BY = bank_jobs()
TURN, TURN_BY = turn_jobs()
BANKS, TURNS = 2, 3


def reads(by, n, who):
    return sum(who in b for b in by[:n + 1])


COPIES = {}
for o in ORDER:
    if o[0] == "cut":
        for b in range(len(BLOCKS)):
            COPIES[o + (b,)] = len(COPIES)
    elif o[0] in ("into", "turn", "carry", "base") or (o[0] == "spread"):
        COPIES[o] = len(COPIES)
        if o[0] == "spread" and o[1] == 0:
            COPIES[o + ("sum",)] = len(COPIES)
RING = 3
LOGITS = {o[1:]: n for n, o in enumerate(x for x in ORDER if x[0] == "logits")}
CUTS = {o[1:]: n for n, o in enumerate(x for x in ORDER if x[0] == "cut")}
ATTENDS = {o[1:]: n for n, o in enumerate(x for x in ORDER if x[0] == "attend")}


def graph_kernel(nc, x, adj_t, w1, w2, w3, u10, u11, u20, u21, gamma, beta, out):
    ctx = ExitStack()
    with ctx:
        def sb(name, shape, dt):
            return ctx.enter_context(nc.sbuf_tensor(name, shape, dt))

        def pb(name, shape, dt):
            return ctx.enter_context(nc.psum_tensor(name, shape, dt))

        def sem(name):
            return ctx.enter_context(nc.semaphore(name))

        adj16 = sb("adj16", [P, 2, NT, N], FP16)
        feat = sb("feat", [P, NT, D], FP32)
        feat16 = feat[:, :, :].bitcast(FP16).rearrange("p t (a d) -> p t a d", a=2)
        mix = sb("mix", [P, NT, D], FP32)
        mix16 = mix[:, :, :].bitcast(FP16).rearrange("p t (a d) -> p t a d", a=2)
        rhs = sb("rhs", [P, NT, D], FP32)
        rhs16 = rhs[:, :, :].bitcast(FP16).rearrange("p t (a d) -> p t a d", a=2)
        xT = sb("xT", [P, DC, 2, N], FP16)
        kq16 = sb("kq16", [DA, 4, NT * P], FP16)
        prob = sb("prob", [P, SLOTS, N], FP32)
        work = sb("work", [P, N], FP32)
        attT = sb("attT", [P, 2, 2, NT * P], FP16)
        w16 = sb("w16", [P, DC, 2, P], FP16)
        w2sb = sb("w2sb", [P, DA], FP32)
        ua16 = sb("ua16", [P, DC, 2, D], FP16)
        ub16 = attT[:, :, :, :].rearrange("p r a n -> p (r a n)")[:, 0:DC * 2 * D].rearrange(
            "p (c a d) -> p c a d", c=DC, a=2)
        ust = sb("ust", [P, DC, D], FP32)
        copy32 = sb("copy32", [P, RING, 512], FP32)
        xnat = sb("xnat", [P, D], FP32)
        ident = sb("ident", [P, P], FP32)
        ones16 = sb("ones16", [P, 2], FP16)
        stage = mix[:, :, :].rearrange("p t d -> p (t d)")[:, 0:4 * N].rearrange("p (r n) -> p r n", r=4)
        wst = prob[:, 0, 0:DC * P].rearrange("p (c n) -> p c n", c=DC)

        bst = sb("bst", [P, 6], FP32)
        mv = sb("mv", [P, NT, 2], FP32)
        lnw = sb("lnw", [P, 6, NT], FP32)
        rinv = sb("rinv", [P, NT], FP32)
        mx = sb("mx", [P, SLOTS], FP32)
        nmx = sb("nmx", [P, 2, SLOTS], FP32)
        zz = sb("zz", [P, 2, SLOTS], FP32)
        zbits = zz[:, :, :].bitcast(INT32)
        tgt = sb("tgt", [P, SLOTS], FP32)
        tg = sb("tg", [P, 2, SLOTS], FP32)
        low = sb("low", [P, 2, SLOTS], FP32)
        high = sb("high", [P, 2, SLOTS], FP32)
        dif = sb("dif", [P, 2, SLOTS], FP32)
        sm = sb("sm", [P, 8, SLOTS], FP32)
        msk = sb("msk", [P, 2, SLOTS], INT32)
        top8 = sb("top8", [P, SLOTS, 8], FP32)
        pre8 = sb("pre8", [P, SLOTS, 8], FP32)
        wk8 = sb("wk8", [P, SLOTS, 8], FP32)
        vcut = sb("vcut", [P, SLOTS], FP32)
        nvcut = sb("nvcut", [P, SLOTS], FP32)
        q1 = sb("q1", [P, SLOTS], FP32)
        zk = sb("zk", [P, SLOTS], FP32)
        rzs = sb("rzs", [P, NT], FP32)
        ymv = sb("ymv", [P, 2], FP32)
        ysm = sb("ysm", [P, 4], FP32)
        ties = [None]
        flag = sb("flag", [P, 32], FP32)
        flagT = sb("flagT", [P, 32], FP32)
        anyf = sb("anyf", [P, 2], FP32)
        anyi = sb("anyi", [P, 2], INT32)
        eq16 = work[:, :].bitcast(FP16)[:, 0:N]
        rk16 = work[:, :].bitcast(FP16)[:, N:2 * N]

        bank = [pb(f"bank{i}", [P, 512], FP32) for i in range(BANKS)]
        turn = [pb(f"turn{i}", [P, 512], FP32) for i in range(TURNS)]
        lg = pb("lg", [P, 3 * 512], FP32)

        s_x = sem("s_x")
        s_adj = [sem(f"s_adj{i}") for i in range(4)]
        s_w = sem("s_w")
        s_u = sem("s_u")
        s_fin = sem("s_fin")
        s_xr = [sem(f"s_xr{i}") for i in range(2)]
        s_out = sem("s_out")
        pool_c = sem("pool_c")
        dve = sem("dve")
        actn = sem("actn")
        pooln = sem("pooln")
        xpad = sem("xpad")
        adj_i = sem("adj_i")
        adj_hi = sem("adj_hi")
        adj_lo = sem("adj_lo")
        stats = sem("stats")
        h_ok = sem("h_ok")
        hhi = sem("hhi")
        hlo = sem("hlo")
        w_hi = sem("w_hi")
        w_lo = sem("w_lo")
        u_hi = sem("u_hi")
        u_lo = sem("u_lo")
        bank_full = sem("bank_full")
        bank_a = sem("bank_a")
        bank_v = sem("bank_v")
        turn_full = sem("turn_full")
        turn_a = sem("turn_a")
        turn_v = sem("turn_v")
        q32 = sem("q32")
        khi = sem("khi")
        copied = sem("copied")
        split = sem("split")
        xn_full = sem("xn_full")
        lg_full = sem("lg_full")
        lg_max = sem("lg_max")
        lg_exp = sem("lg_exp")
        gin = sem("gin")
        gex = sem("gex")
        guess = sem("guess")
        a_ready = sem("a_ready")
        y_ok = sem("y_ok")
        yn = sem("yn")
        xb = sem("xb")
        o_ok = sem("o_ok")
        rs_one = sem("rs_one")
        rs_raw = sem("rs_raw")
        rs_ok = sem("rs_ok")

        block = ctx.enter_context(nc.Block())
        W_IN = [u11, u10, u21, u20]

        @block.sync
        def _(sp):
            sp.dma_start(rhs[:, 0:NT - 1, :], x[0:(NT - 1) * P, :].rearrange("(t p) d -> p t d", p=P)).then_inc(s_x, 16)
            sp.wait_ge(xpad, 1)
            sp.dma_start(rhs[0:rows(NT - 1), NT - 1, :], x[(NT - 1) * P:N, :]).then_inc(s_x, 16)
            sp.dma_start(wst[:, :, 0:DA], w3.rearrange("(c p) n -> p c n", p=P)).then_inc(s_w, 16)
            sp.dma_start(wst[:, :, DA:P], w1.rearrange("(c p) n -> p c n", p=P)).then_inc(s_w, 16)
            sp.dma_start(w2sb[DA:P, :], w2[:, :]).then_inc(s_w, 16)
            for n in range(4):
                if n == 0:
                    sp.dma_start(ust[:, :, :], W_IN[0].rearrange("(c p) n -> p c n", p=P)).then_inc(s_u, 16)
                sp.dma_start(stage[0:rows(n), n, :], adj_t[n * P:n * P + rows(n), :]).then_inc(s_adj[n % 4], 16)
            for n in range(4, NT):
                sp.wait_ge(adj_hi, n - 3)
                sp.wait_ge(adj_lo, n - 3)
                sp.dma_start(stage[0:rows(n), n % 4, :], adj_t[n * P:n * P + rows(n), :]).then_inc(s_adj[n % 4], 16)
            for n in range(1, 4):
                sp.wait_ge(u_hi, n)
                sp.wait_ge(u_lo, n)
                sp.dma_start(ust[:, :, :], W_IN[n].rearrange("(c p) n -> p c n", p=P)).then_inc(s_u, 16)
            sp.wait_ge(u_hi, 4)
            sp.wait_ge(u_lo, 4)
            sp.dma_start(ust[:, 2, :], gamma.rearrange("(a n) -> a n", a=1).broadcast_to((P, D))).then_inc(s_fin, 16)
            sp.dma_start(ust[:, 3, :], beta.rearrange("(a n) -> a n", a=1).broadcast_to((P, D))).then_inc(s_fin, 16)
            for t in range(NT):
                if t >= 2:
                    sp.wait_ge(o_ok, t - 1)
                sp.dma_start(ust[0:rows(t), t % 2, :], x[t * P:t * P + rows(t), :]).then_inc(s_xr[t % 2], 16)
                if t >= 1:
                    sp.wait_ge(o_ok, t)
                    sp.dma_start(out[(t - 1) * P:t * P, :], feat[:, t - 1, :]).then_inc(s_out, 16)
            sp.wait_ge(o_ok, NT)
            sp.dma_start(out[(NT - 1) * P:N, :], feat[0:rows(NT - 1), NT - 1, :]).then_inc(s_out, 16)
            sp.wait_ge(s_out, 16 * NT)

        @block.gpsimd
        def _(pool):
            steps = [0]

            def did(ins):
                steps[0] += 1
                ins.then_inc(pooln, 1)

            def settle():
                pool.wait_ge(pooln, steps[0])

            did(nc.gpsimd.memset(ident[:, :], 0.0))
            nc.gpsimd.memset(ones16[:, :], 1.0).then_inc(pool_c, 1)
            settle()
            nc.gpsimd.affine_select(out=ident[:, :], in_=ident[:, :], compare_op=ALU.not_equal, fill=1.0, base=0,
                                    pattern=[[-1, P]], channel_multiplier=1).then_inc(pool_c, 1)

            def lo_half(o, dst, hi, width):
                n = COPIES[o]
                pool.wait_ge(copied, n + 1)
                nc.gpsimd.tensor_tensor(out=dst, in0=copy32[:, n % RING, 0:width], in1=hi,
                                        op=ALU.subtract).then_inc(split, 1)

            def weights_lo(n, dst):
                pool.wait_ge(u_hi, n + 1)
                for c in range(DC):
                    last = nc.gpsimd.tensor_tensor(out=dst[:, c, 1, :], in0=ust[:, c, :], in1=dst[:, c, 0, :],
                                                   op=ALU.subtract)
                last.then_inc(u_lo, 1)

            for o in ORDER:
                if o[0] == "prep":
                    weights_lo(0, ub16)
                    weights_lo(1, ua16)
                elif o[0] == "weights":
                    weights_lo(o[1], ua16 if o[1] == 2 else ub16)
                elif o[0] in ("into", "carry"):
                    lo_half(o, rhs16[:, o[1], 1, :], rhs16[:, o[1], 0, :], D)
                elif o[0] == "turn":
                    t = o[1]
                    n = COPIES[o]
                    pool.wait_ge(copied, n + 1)
                    nc.gpsimd.tensor_tensor(
                        out=xT[:, :, 1, t * P:t * P + rows(t)],
                        in0=copy32[:, n % RING, :].rearrange("p (c n) -> p c n", c=DC)[:, :, 0:rows(t)],
                        in1=xT[:, :, 0, t * P:t * P + rows(t)], op=ALU.subtract).then_inc(split, 1)
                elif o[0] == "cut":
                    r = CUTS[o[1:]] % 2
                    for b, blocks in enumerate(BLOCKS):
                        a, e = blocks[0] * P, (blocks[-1] + 1) * P
                        lo_half(o + (b,), attT[:, r, 1, a:e], attT[:, r, 0, a:e], e - a)
                elif o[0] == "spread" and o[1] == 0:
                    t = o[2]
                    n, m = COPIES[o], COPIES[o + ("sum",)]
                    pool.wait_ge(copied, n + 1)
                    if m >= RING:
                        pool.wait_ge(split, m - RING + 1)
                    did(nc.gpsimd.tensor_tensor(out=copy32[:, m % RING, :], in0=copy32[:, n % RING, :],
                                                in1=mix[:, t, :], op=ALU.add))
                    settle()
                    nc.gpsimd.sem_inc(split, 1)
                    lo_half(o + ("sum",), mix16[:, t, 1, :], mix16[:, t, 0, :], D)
                elif o[0] == "spread":
                    t = o[2]
                    n = COPIES[o]
                    pool.wait_ge(copied, n + 1)
                    nc.gpsimd.tensor_tensor(out=feat[:, t, :], in0=feat[:, t, :], in1=copy32[:, n % RING, :],
                                            op=ALU.add).then_inc(split, 1)
                elif o[0] == "base":
                    t = o[1]
                    n = COPIES[o]
                    pool.wait_ge(copied, n + 1)
                    did(nc.gpsimd.tensor_tensor(out=copy32[:, n % RING, :], in0=copy32[:, n % RING, :],
                                                in1=feat16[:, t, 0, :], op=ALU.add))
                    settle()
                    did(nc.gpsimd.tensor_tensor(out=copy32[:, n % RING, :], in0=copy32[:, n % RING, :],
                                                in1=feat16[:, t, 1, :], op=ALU.add))
                    settle()
                    nc.gpsimd.tensor_copy(feat[:, t, :], copy32[:, n % RING, :]).then_inc(split, 1)
                elif o[0] == "norm":
                    t = o[1]
                    if t == 0:
                        pool.wait_ge(s_fin, 32)
                    pool.wait_ge(s_xr[t % 2], 16 * (t // 2 + 1))
                    r_ = rows(t)
                    did(nc.gpsimd.tensor_tensor(out=ust[0:r_, t % 2, :], in0=ust[0:r_, t % 2, :],
                                                in1=ust[0:r_, 3, :], op=ALU.add))
                    pool.wait_ge(yn, t + 1)
                    did(nc.gpsimd.tensor_tensor(out=feat[0:r_, t, :], in0=feat[0:r_, t, :],
                                                in1=ust[0:r_, 2, :], op=ALU.mult))
                    settle()
                    nc.gpsimd.tensor_tensor(out=feat[0:r_, t, :], in0=feat[0:r_, t, :],
                                            in1=ust[0:r_, t % 2, :], op=ALU.add).then_inc(o_ok, 1)

        @block.scalar
        def _(act):
            steps = [0]

            def did(ins):
                steps[0] += 1
                ins.then_inc(actn, 1)

            def settle():
                act.wait_ge(actn, steps[0])

            def hi_and_copy(o, src, scale, hi, cp, read):
                n = COPIES[o]
                if n >= RING:
                    act.wait_ge(split, n - RING + 1)
                nc.scalar.activation(hi, src, ACT.Copy, scale=scale).then_inc(actn, 1)
                steps[0] += 1
                did(nc.scalar.activation(cp, src, ACT.Copy, scale=scale))
                settle()
                nc.scalar.sem_inc(copied, 1)
                if read is not None:
                    nc.scalar.sem_inc(read, 1)

            def copy_only(o, src, scale, read):
                n = COPIES[o]
                if n >= RING:
                    act.wait_ge(split, n - RING + 1)
                did(nc.scalar.activation(copy32[:, n % RING, :], src, ACT.Copy, scale=scale))
                settle()
                nc.scalar.sem_inc(copied, 1)
                nc.scalar.sem_inc(read, 1)

            def weights_hi(n, dst):
                act.wait_ge(s_u, 16 * (n + 1))
                did(nc.scalar.activation(dst[:, :, 0, :], ust[:, :, :], ACT.Copy, scale=SC_U))
                settle()
                nc.scalar.activation(ust[:, :, :], ust[:, :, :], ACT.Copy, scale=SC_U).then_inc(u_hi, 1)

            for o in ORDER:
                if o[0] == "prep":
                    act.wait_ge(s_w, 48)
                    nc.scalar.activation(w16[:, :, 0, :], wst[:, :, :], ACT.Copy, scale=SC_U).then_inc(w_hi, 1)
                    act.wait_ge(stats, 1)
                    for t in range(NT):
                        did(nc.scalar.activation(rhs[:, t, :], rhs[:, t, :], ACT.Relu, scale=lnw[:, 2, t:t + 1],
                                                 bias=lnw[:, 4, t:t + 1]))
                        settle()
                        nc.scalar.sem_inc(h_ok, 1)
                        nc.scalar.activation(feat16[:, t, 0, :], rhs[:, t, :], ACT.Copy, scale=SC_X).then_inc(hhi, 1)
                    for t in range(NT):
                        n = TURN[("ht", t)]
                        act.wait_ge(turn_full, n + 1)
                        nc.scalar.activation(xT[:, :, 0, t * P:t * P + rows(t)],
                                             turn[n % TURNS][:, :].rearrange("p (c n) -> p c n", c=DC)[:, :, 0:rows(t)],
                                             ACT.Copy, scale=SC_X).then_inc(turn_a, 1)
                    for n in range(NT):
                        act.wait_ge(adj_i, n + 1)
                        nc.scalar.activation(adj16[:, 0, n, :], stage[:, n % 4, :], ACT.Copy,
                                             scale=SC_S).then_inc(adj_hi, 1)
                    weights_hi(0, ub16)
                    weights_hi(1, ua16)
                elif o[0] == "weights":
                    last = BANK[("first", NT - 1)] if o[1] == 2 else BANK[("attend", 0, NT - 1)]
                    act.wait_ge(bank_full, last + 1)
                    if o[1] == 3:
                        act.wait_ge(split, COPIES[("cut", 0, NT - 1, len(BLOCKS) - 1)] + 1)
                    weights_hi(o[1], ua16 if o[1] == 2 else ub16)
                elif o[0] == "qk":
                    s, c = o[1:]
                    n = BANK[o]
                    a, w = CHUNKS[c]
                    act.wait_ge(bank_full, n + 1)
                    nc.scalar.activation(kq16[:, 0, a:a + w], bank[n % BANKS][0:DA, 0:w], ACT.Copy,
                                         scale=SC_K / (SC_X * SC_U)).then_inc(khi, 1)
                    did(nc.scalar.activation(work[DA:P, a:a + w], bank[n % BANKS][DA:P, 0:w], ACT.Copy,
                                             scale=1.0 / (SC_X * SC_U)))
                    settle()
                    nc.scalar.sem_inc(q32, 1)
                    nc.scalar.sem_inc(bank_a, 1)
                elif o[0] == "q2":
                    s, c = o[1:]
                    n = TURN[o]
                    a, w = CHUNKS[c]
                    act.wait_ge(turn_full, n + 1)
                    nc.scalar.activation(kq16[:, 2, a:a + w], turn[n % TURNS][0:DA, 0:w], ACT.Copy,
                                         scale=SC_K).then_inc(turn_a, 1)
                elif o[0] == "logits":
                    s, t = o[1:]
                    i = t % SLOTS
                    n = LOGITS[o[1:]]
                    act.wait_ge(lg_max, n + 1)
                    did(nc.scalar.activation(prob[:, i, :], lg[:, 0:N], ACT.Exp, scale=1.0 / SC_K ** 2,
                                             bias=nmx[:, 0, i:i + 1], accum_out=zz[:, 0, i:i + 1]))
                    settle()
                    did(nc.scalar.activation(lg[:, 0:N], lg[:, 0:N], ACT.Exp, scale=0.5 / SC_K ** 2,
                                             bias=nmx[:, 1, i:i + 1], accum_out=zz[:, 1, i:i + 1]))
                    settle()
                    nc.scalar.sem_inc(lg_exp, 1)
                elif o[0] == "select":
                    s, g = o[1:]
                    k = len(GROUPS[g])
                    n = s * len(GROUPS) + g
                    act.wait_ge(gin, n + 1)
                    nc.scalar.activation(tg[:, 0, 0:k], sm[:, 0, 0:k], ACT.Exp).then_inc(guess, 1)
                elif o[0] in ("into", "carry"):
                    n = BANK[o]
                    if o == ("into", 0):
                        act.wait_ge(hlo, NT)
                    act.wait_ge(bank_full, n + 1)
                    hi_and_copy(o, bank[n % BANKS][:, :], 1.0 / SC_U, rhs16[:, o[1], 0, :],
                                copy32[:, COPIES[o] % RING, :], bank_a)
                elif o[0] == "first":
                    n = BANK[o]
                    if o[1] == 0:
                        act.wait_ge(adj_lo, NT)
                    act.wait_ge(bank_full, n + 1)
                    did(nc.scalar.activation(mix[:, o[1], :], bank[n % BANKS][:, :], ACT.Copy, scale=1.0 / SC_U))
                    settle()
                    nc.scalar.sem_inc(bank_a, 1)
                elif o[0] == "rowsum":
                    n = BANK[o]
                    r_ = rows(NT - 1)
                    act.wait_ge(rs_one, 1)
                    act.wait_ge(bank_full, n + 1)
                    did(nc.scalar.activation(rinv[:, 0:NT - 1], bank[n % BANKS][:, 0:NT - 1], ACT.Copy,
                                             scale=1.0 / SC_S))
                    did(nc.scalar.activation(rinv[0:r_, NT - 1:NT], bank[n % BANKS][0:r_, NT - 1:NT], ACT.Copy,
                                             scale=1.0 / SC_S))
                    settle()
                    nc.scalar.sem_inc(bank_a, 1)
                    nc.scalar.sem_inc(rs_raw, 1)
                elif o[0] == "base":
                    n = BANK[o]
                    act.wait_ge(bank_full, n + 1)
                    copy_only(o, bank[n % BANKS][:, :], 1.0 / SC_U, bank_a)
                elif o[0] == "spread":
                    s, t = o[1:]
                    n = BANK[o]
                    if s == 0 and t == 0:
                        act.wait_ge(rs_ok, 1)
                    act.wait_ge(bank_full, n + 1)
                    copy_only(o, bank[n % BANKS][:, :], rinv[:, t:t + 1], bank_a)
                    if s == 0:
                        m = COPIES[o + ("sum",)]
                        act.wait_ge(split, m)
                        did(nc.scalar.activation(mix16[:, t, 0, :], copy32[:, m % RING, :], ACT.Copy))
                        settle()
                        nc.scalar.sem_inc(copied, 1)
                elif o[0] == "cut":
                    s, t = o[1:]
                    r = CUTS[o[1:]] % 2
                    if s == 0 and t == 0:
                        act.wait_ge(bank_full, BANK[("first", NT - 1)] + 1)
                    if CUTS[o[1:]] >= 2:
                        k = CUTS[o[1:]] - 2
                        prev = ("attend", k // NT, k % NT)
                        act.wait_ge(bank_full, BANK[prev] + 1)
                    for b, blocks in enumerate(BLOCKS):
                        n = TURN[o + (b,)]
                        a, e = blocks[0] * P, (blocks[-1] + 1) * P
                        act.wait_ge(turn_full, n + 1)
                        hi_and_copy(o + (b,), turn[n % TURNS][:, 0:e - a], SC_P, attT[:, r, 0, a:e],
                                    copy32[:, COPIES[o + (b,)] % RING, 0:e - a], turn_a)
                elif o[0] == "attend" and o[1] == 0:
                    s, t = o[1:]
                    n = BANK[o]
                    act.wait_ge(bank_full, n + 1)
                    if t > 0:
                        act.wait_ge(turn_full, TURN[("turn", t - 1)] + 1)
                    did(nc.scalar.activation(xnat[:, :], bank[n % BANKS][:, :], ACT.Copy, scale=rzs[:, t:t + 1]))
                    settle()
                    nc.scalar.sem_inc(xn_full, 1)
                    nc.scalar.sem_inc(bank_a, 1)
                elif o[0] == "turn":
                    t = o[1]
                    n = TURN[o]
                    act.wait_ge(turn_full, n + 1)
                    src = turn[n % TURNS][:, :].rearrange("p (c n) -> p c n", c=DC)[:, :, 0:rows(t)]
                    cp = copy32[:, COPIES[o] % RING, :].rearrange("p (c n) -> p c n", c=DC)[:, :, 0:rows(t)]
                    hi_and_copy(o, src, SC_X, xT[:, :, 0, t * P:t * P + rows(t)], cp, turn_a)

        @block.vector
        def _(v):
            steps = [0]

            def did(ins):
                steps[0] += 1
                return ins.then_inc(dve, 1)

            def settle():
                v.wait_ge(dve, steps[0])

            def step(ins):
                did(ins)
                settle()

            def rsqrt(y, r, w):
                step(nc.vector.tensor_scalar(r.bitcast(INT32), y.bitcast(INT32), -0.5, RSQRT_BITS, ALU.mult, ALU.add))
                for _ in range(4):
                    step(nc.vector.tensor_tensor(w, r, r, ALU.mult))
                    step(nc.vector.tensor_tensor(w, w, y, ALU.mult))
                    step(nc.vector.tensor_scalar(w, w, -0.5, 1.5, ALU.mult, ALU.add))
                    step(nc.vector.tensor_tensor(r, r, w, ALU.mult))

            def mass(i, cut, dst, sig=None):
                return nc.vector.scalar_tensor_tensor(out=work[:, :], in0=prob[:, i, :], scalar=cut, in1=prob[:, i, :],
                                                      op0=ALU.is_ge, op1=ALU.mult, accum_out=dst)

            def window(i, fence, done):
                fence(nc.vector.scalar_tensor_tensor(out=work[:, :], in0=prob[:, i, :], scalar=high[:, 0, i:i + 1],
                                                     in1=prob[:, i, :], op0=ALU.is_lt, op1=ALU.mult))
                fence(nc.vector.max(top8[:, i, :], work[:, :]))
                done(mass(i, top8[:, i, 7:8], tg[:, 1, i:i + 1]))

            def lower_bound_moves(k, fence):
                K = slice(0, k)
                fence(nc.vector.tensor_tensor(msk[:, 0, K], tg[:, 1, K], tgt[:, K], ALU.is_lt))
                fence(nc.vector.tensor_copy(tg[:, 0, K], top8[:, K, 7]))
                fence(nc.vector.tensor_copy(msk[:, 1, K], msk[:, 0, K]))
                fence(nc.vector.copy_predicated(high[:, :, K], msk[:, :, K], tg[:, :, K]))

            def open_rows(k, fence):
                fence(nc.vector.tensor_tensor(sm[:, 0, 0:k], tg[:, 1, 0:k], tgt[:, 0:k], ALU.is_lt))
                fence(nc.vector.tensor_reduce(flag[:, 0:1], sm[:, 0, 0:k], AX.X, ALU.max))
                any_row(fence)

            def any_row(fence):
                fence(nc.vector.transpose(flagT[:, :], flag[:, :]))
                fence(nc.vector.tensor_reduce(anyf[:, 0:1], flagT[:, :], AX.X, ALU.max))
                fence(nc.vector.tensor_copy(anyi[:, 0:1], anyf[:, 0:1]))

            nc.vector.memset(rhs[64:P, NT - 1, :], 0.0).then_inc(xpad, 1)
            v.wait_ge(s_x, 32)
            v.wait_ge(xpad, 1)
            for t in range(NT):
                step(nc.vector.bn_stats(bst[:, :], rhs[:, t, :]))
                step(nc.vector.bn_aggr(mv[:, t, :], bst[:, :]))
            step(nc.vector.tensor_scalar(lnw[:, 0, :], mv[:, :, 1], LN_EPS, None, ALU.add))
            rsqrt(lnw[:, 0, :], lnw[:, 2, :], lnw[:, 3, :])
            v.wait_ge(s_w, 48)
            v.wait_ge(w_hi, 1)
            nc.vector.scalar_tensor_tensor(out=w16[:, :, 1, :], in0=wst[:, :, :], scalar=SC_U, in1=w16[:, :, 0, :],
                                           op0=ALU.mult, op1=ALU.subtract).then_inc(w_lo, 1)
            step(nc.vector.scalar_tensor_tensor(out=lnw[:, 4, :], in0=mv[:, :, 0], scalar=-1.0, in1=lnw[:, 2, :],
                                                op0=ALU.mult, op1=ALU.mult))
            nc.vector.sem_inc(stats, 1)
            nc.vector.memset(rinv[:, :], 1.0).then_inc(rs_one, 1)
            step(nc.vector.memset(flag[:, :], 0.0))
            step(nc.vector.memset(anyf[:, :], 0.0))
            for t in range(NT):
                v.wait_ge(hhi, t + 1)
                nc.vector.scalar_tensor_tensor(out=feat16[:, t, 1, :], in0=rhs[:, t, :], scalar=SC_X,
                                               in1=feat16[:, t, 0, :], op0=ALU.mult, op1=ALU.subtract).then_inc(hlo, 1)
                n = TURN[("ht", t)]
                v.wait_ge(turn_a, n + 1)
                nc.vector.scalar_tensor_tensor(out=xT[:, :, 1, t * P:t * P + rows(t)],
                                               in0=turn[n % TURNS][:, :].rearrange("p (c n) -> p c n", c=DC)[:, :, 0:rows(t)],
                                               scalar=SC_X, in1=xT[:, :, 0, t * P:t * P + rows(t)],
                                               op0=ALU.mult, op1=ALU.subtract).then_inc(turn_v, 1)
            v.wait_ge(pool_c, 2)
            for n in range(NT + 1):
                if n < NT:
                    v.wait_ge(s_adj[n % 4], 16 * (n // 4 + 1))
                    a, r_ = n * P, rows(n)
                    nc.vector.tensor_tensor(stage[0:r_, n % 4, a:a + r_], stage[0:r_, n % 4, a:a + r_],
                                            ident[0:r_, 0:r_], ALU.add).then_inc(adj_i, 1)
                if n > 0:
                    v.wait_ge(adj_hi, n)
                    nc.vector.scalar_tensor_tensor(out=adj16[:, 1, n - 1, :], in0=stage[:, (n - 1) % 4, :], scalar=SC_S,
                                                   in1=adj16[:, 0, n - 1, :], op0=ALU.mult,
                                                   op1=ALU.subtract).then_inc(adj_lo, 1)

            for o in ORDER:
                if o[0] == "qk":
                    s, c = o[1:]
                    n = BANK[o]
                    a, w = CHUNKS[c]
                    v.wait_ge(khi, s * len(CHUNKS) + c + 1)
                    nc.vector.scalar_tensor_tensor(out=kq16[:, 1, a:a + w], in0=bank[n % BANKS][0:DA, 0:w],
                                                   scalar=SC_K / (SC_X * SC_U), in1=kq16[:, 0, a:a + w],
                                                   op0=ALU.mult, op1=ALU.subtract).then_inc(bank_v, 1)
                elif o[0] == "q2":
                    s, c = o[1:]
                    n = TURN[o]
                    a, w = CHUNKS[c]
                    v.wait_ge(turn_a, n + 1)
                    lo = nc.vector.scalar_tensor_tensor(out=kq16[:, 3, a:a + w], in0=turn[n % TURNS][0:DA, 0:w],
                                                        scalar=SC_K, in1=kq16[:, 2, a:a + w],
                                                        op0=ALU.mult, op1=ALU.subtract)
                    if c == len(CHUNKS) - 1:
                        step(lo)
                        pad = NT * P - N
                        lo = nc.vector.tensor_copy(kq16[:, 2:4, N:N + pad], kq16[:, 2:4, N - pad:N])
                    lo.then_inc(turn_v, 1)
                elif o[0] == "rowsum":
                    v.wait_ge(rs_raw, 1)
                    step(nc.vector.tensor_scalar(rinv[:, :], rinv[:, :], 1e-12, None, ALU.max))
                    step(nc.vector.reciprocal(rinv[:, :], rinv[:, :]))
                    step(nc.vector.tensor_scalar(rinv[:, :], rinv[:, :], 1.0 / SC_S, None, ALU.mult))
                    nc.vector.sem_inc(rs_ok, 1)
                elif o[0] == "logits":
                    s, t = o[1:]
                    i = t % SLOTS
                    n = LOGITS[o[1:]]
                    v.wait_ge(lg_full, n + 1)
                    step(nc.vector.reduce_max(mx[:, i:i + 1], lg[:, 0:N], AX.X))
                    did(nc.vector.tensor_scalar(nmx[:, 0, i:i + 1], mx[:, i:i + 1], -1.0 / SC_K ** 2, None, ALU.mult))
                    did(nc.vector.tensor_scalar(nmx[:, 1, i:i + 1], mx[:, i:i + 1], -0.5 / SC_K ** 2, None, ALU.mult))
                    settle()
                    nc.vector.sem_inc(lg_max, 1)
                elif o[0] == "select":
                    s, g = o[1:]
                    group = GROUPS[g]
                    k = len(group)
                    K = slice(0, k)
                    ng = s * len(GROUPS) + g
                    v.wait_ge(lg_exp, s * NT + group[-1] + 1)
                    step(nc.vector.tensor_scalar(sm[:, 1, K], zbits[:, 0, K], GUESS[0] * LOG_BITS,
                                                 GUESS[2] - (GUESS[0] + GUESS[1]) * LOG_ONE, ALU.mult, ALU.add))
                    step(nc.vector.scalar_tensor_tensor(out=sm[:, 0, K], in0=zbits[:, 1, K], scalar=GUESS[1] * LOG_BITS,
                                                        in1=sm[:, 1, K],
                                                        op0=ALU.mult, op1=ALU.add))
                    nc.vector.sem_inc(gin, 1)
                    did(nc.vector.tensor_scalar(tgt[:, K], zz[:, 0, K], P_TOP, None, ALU.mult))
                    did(nc.vector.memset(high[:, 0, K], HI0))
                    did(nc.vector.memset(high[:, 1, K], 0.0))
                    did(nc.vector.memset(low[:, 0, K], 0.0))
                    did(nc.vector.tensor_copy(low[:, 1, K], zz[:, 0, K]))
                    v.wait_ge(guess, ng + 1)
                    step(nc.vector.tensor_scalar(tg[:, 0, K], tg[:, 0, K], 1.0, None, ALU.min))
                    for e in range(EVALS[s]):
                        for i in range(k):
                            step(mass(i, tg[:, 0, i:i + 1], tg[:, 1, i:i + 1]))
                        settle()
                        did(nc.vector.tensor_tensor(msk[:, 0, K], tg[:, 1, K], tgt[:, K], ALU.is_ge))
                        did(nc.vector.tensor_tensor(msk[:, 1, K], tg[:, 1, K], tgt[:, K], ALU.is_ge))
                        settle()
                        step(nc.vector.copy_predicated(low[:, :, K], msk[:, :, K], tg[:, :, K]))
                        did(nc.vector.tensor_tensor(msk[:, 0, K], tg[:, 1, K], tgt[:, K], ALU.is_lt))
                        did(nc.vector.tensor_tensor(msk[:, 1, K], tg[:, 1, K], tgt[:, K], ALU.is_lt))
                        settle()
                        step(nc.vector.copy_predicated(high[:, :, K], msk[:, :, K], tg[:, :, K]))
                        if e == EVALS[s] - 1:
                            break
                        step(nc.vector.tensor_tensor(dif[:, :, K], high[:, :, K], low[:, :, K], ALU.subtract))
                        did(nc.vector.tensor_tensor(sm[:, 1, K], low[:, 1, K], tgt[:, K], ALU.subtract))
                        step(nc.vector.reciprocal(sm[:, 0, K], dif[:, 1, K]))
                        step(nc.vector.scalar_tensor_tensor(out=sm[:, 1, K], in0=low[:, 0, K], scalar=4.0, in1=sm[:, 1, K],
                                                            op0=ALU.mult, op1=ALU.add))
                        step(nc.vector.scalar_tensor_tensor(out=sm[:, 1, K], in0=sm[:, 1, K], scalar=-1.0, in1=sm[:, 0, K],
                                                            op0=ALU.mult, op1=ALU.mult))
                        step(nc.vector.tensor_scalar(sm[:, 1, K], sm[:, 1, K], 0.02, 0.98, ALU.max, ALU.min))
                        step(nc.vector.tensor_tensor(sm[:, 1, K], sm[:, 1, K], dif[:, 0, K], ALU.mult))
                        step(nc.vector.tensor_tensor(tg[:, 0, K], sm[:, 1, K], low[:, 0, K], ALU.add))
                    for w in range(WINDOWS[s]):
                        if w:
                            lower_bound_moves(k, step)
                        for i in range(k):
                            window(i, step, step)
                    open_rows(k, step)
                    def some_row_is_open():
                        q = [v.value_load(anyi[32 * q:32 * q + 1, 0:1], min_val=0, max_val=1) for q in range(4)]
                        return q[0] + q[1] + q[2] + q[3] > 0

                    def fence(ins):
                        nc.vector.drain()

                    with v.While(some_row_is_open):
                        lower_bound_moves(k, fence)
                        for i in range(k):
                            window(i, fence, fence)
                        open_rows(k, fence)
                    for i in range(k):
                        did(nc.vector.tensor_tensor_scan(pre8[:, i, :], top8[:, i, :], top8[:, i, :],
                                                         high[:, 1, i:i + 1], ALU.add, ALU.max))
                    settle()
                    tgt8 = tgt[:, K].rearrange("p (k a) -> p k a", a=1).broadcast_to((P, k, 8))
                    step(nc.vector.tensor_tensor(wk8[:, K, :], pre8[:, K, :], tgt8, ALU.is_ge))
                    step(nc.vector.tensor_tensor(wk8[:, K, :], wk8[:, K, :], top8[:, K, :], ALU.mult))
                    step(nc.vector.tensor_reduce(vcut[:, K], wk8[:, K, :], AX.X, ALU.max))
                    step(nc.vector.tensor_tensor(vcut[:, K], vcut[:, K], top8[:, K, 7], ALU.max))
                    v8 = vcut[:, K].rearrange("p (k a) -> p k a", a=1).broadcast_to((P, k, 8))
                    did(nc.vector.tensor_scalar(nvcut[:, K], vcut[:, K], -1.0, None, ALU.mult))
                    step(nc.vector.tensor_tensor(wk8[:, K, :], top8[:, K, :], v8, ALU.is_gt))
                    step(nc.vector.tensor_tensor(wk8[:, K, :], wk8[:, K, :], top8[:, K, :], ALU.mult))
                    step(nc.vector.tensor_reduce(sm[:, 0, K], wk8[:, K, :], AX.X, ALU.add))
                    step(nc.vector.tensor_tensor(sm[:, 0, K], sm[:, 0, K], high[:, 1, K], ALU.add))
                    step(nc.vector.tensor_tensor(sm[:, 1, K], tgt[:, K], sm[:, 0, K], ALU.subtract))
                    step(nc.vector.reciprocal(sm[:, 2, K], vcut[:, K]))
                    step(nc.vector.tensor_tensor(sm[:, 1, K], sm[:, 1, K], sm[:, 2, K], ALU.mult))
                    step(nc.vector.tensor_scalar(q1[:, K], sm[:, 1, K], 0.5, 1.0, ALU.max, ALU.add))
                    step(nc.vector.tensor_tensor(wk8[:, K, :], top8[:, K, :], v8, ALU.is_equal))
                    step(nc.vector.tensor_reduce(sm[:, 3, K], wk8[:, K, :], AX.X, ALU.add))
                    step(nc.vector.tensor_tensor(sm[:, 4, K], tg[:, 1, K], pre8[:, K, 7], ALU.subtract))
                    step(nc.vector.tensor_tensor(sm[:, 4, K], sm[:, 4, K], sm[:, 2, K], ALU.mult))
                    step(nc.vector.tensor_tensor(sm[:, 4, K], sm[:, 4, K], wk8[:, K, 7], ALU.mult))
                    step(nc.vector.tensor_tensor(sm[:, 3, K], sm[:, 3, K], sm[:, 4, K], ALU.add))
                    step(nc.vector.tensor_scalar(sm[:, 3, K], sm[:, 3, K], ROUND_INT, -ROUND_INT, ALU.add, ALU.add))
                    step(nc.vector.tensor_tensor(sm[:, 3, K], sm[:, 3, K], q1[:, K], ALU.is_ge))
                    step(nc.vector.tensor_reduce(flag[:, 0:1], sm[:, 3, K], AX.X, ALU.max))
                    any_row(step)
                    ties[0] = [v.value_load(anyi[32 * q:32 * q + 1, 0:1], min_val=0, max_val=1) for q in range(4)]
                elif o[0] == "cut":
                    s, t = o[1:]
                    i = t % SLOTS
                    step(nc.vector.scalar_tensor_tensor(out=prob[:, i, :], in0=prob[:, i, :], scalar=vcut[:, i:i + 1],
                                                        in1=prob[:, i, :], op0=ALU.is_ge, op1=ALU.mult,
                                                        accum_out=zk[:, i:i + 1]))
                    q = ties[0]
                    with v.If(q[0] + q[1] + q[2] + q[3] > 0):
                        nc.vector.tensor_scalar(eq16, prob[:, i, :], vcut[:, i:i + 1], None, ALU.is_equal)
                        nc.vector.drain()
                        nc.vector.tensor_tensor_scan(rk16, eq16, eq16, 0.0, ALU.add, ALU.max)
                        nc.vector.drain()
                        nc.vector.scalar_tensor_tensor(out=eq16, in0=rk16, scalar=q1[:, i:i + 1], in1=eq16,
                                                       op0=ALU.is_ge, op1=ALU.mult)
                        nc.vector.drain()
                        nc.vector.scalar_tensor_tensor(out=prob[:, i, :], in0=eq16, scalar=nvcut[:, i:i + 1],
                                                       in1=prob[:, i, :], op0=ALU.mult, op1=ALU.add,
                                                       accum_out=zk[:, i:i + 1])
                        nc.vector.drain()
                    did(nc.vector.reciprocal(rzs[:, t:t + 1], zk[:, i:i + 1]))
                    settle()
                    step(nc.vector.tensor_scalar(rzs[:, t:t + 1], rzs[:, t:t + 1],
                                                 1.0 / (SC_P * SC_X) if s == 0 else 1.0 / SC_P, None, ALU.mult))
                    nc.vector.sem_inc(a_ready, 1)
                elif o[0] == "attend" and o[1] == 1:
                    t = o[2]
                    n = BANK[o]
                    v.wait_ge(bank_full, n + 1)
                    v.wait_ge(split, COPIES[("spread", 1, t)] + 1)
                    step(nc.vector.scalar_tensor_tensor(out=feat[:, t, :], in0=bank[n % BANKS][:, :],
                                                        scalar=rzs[:, t:t + 1], in1=feat[:, t, :],
                                                        op0=ALU.mult, op1=ALU.add))
                    nc.vector.sem_inc(bank_v, 1)
                elif o[0] == "norm":
                    t = o[1]
                    step(nc.vector.bn_stats(bst[:, :], feat[:, t, :]))
                    step(nc.vector.bn_aggr(ymv[:, :], bst[:, :]))
                    step(nc.vector.tensor_scalar(ysm[:, 0:1], ymv[:, 1:2], LN_EPS * SC_X ** 2, None, ALU.add))
                    rsqrt(ysm[:, 0:1], ysm[:, 2:3], ysm[:, 3:4])
                    nc.vector.tensor_scalar(feat[:, t, :], feat[:, t, :], ymv[:, 0:1], ysm[:, 2:3],
                                            ALU.subtract, ALU.mult).then_inc(yn, 1)

        @block.tensor
        def _(pe):
            def three(dst, l_hi, l_lo, r_hi, r_lo, first, last):
                nc.tensor.matmul(dst, l_hi, r_hi, start=first, stop=False)
                nc.tensor.matmul(dst, l_hi, r_lo, start=False, stop=False)
                return nc.tensor.matmul(dst, l_lo, r_hi, start=False, stop=last)

            def free(jobs_by, n, ring, sem_a, sem_v):
                if n >= ring:
                    for who, sm_ in (("a", sem_a), ("v", sem_v)):
                        if who in jobs_by[n - ring]:
                            pe.wait_ge(sm_, reads(jobs_by, n - ring, who))

            pe.wait_ge(pool_c, 2)
            for t in range(NT):
                n = TURN[("ht", t)]
                pe.wait_ge(h_ok, t + 1)
                free(TURN_BY, n, TURNS, turn_a, turn_v)
                r_ = rows(t)
                for c in range(DC):
                    last = nc.tensor.transpose(turn[n % TURNS][:, c * P:c * P + r_], rhs[0:r_, t, c * P:(c + 1) * P],
                                               ident[0:r_, 0:r_])
                last.then_inc(turn_full, 1)

            for o in ORDER:
                if o[0] == "qk":
                    s, c = o[1:]
                    n = BANK[o]
                    a, w = CHUNKS[c]
                    if s == 0 and c == 0:
                        pe.wait_ge(w_lo, 1)
                        pe.wait_ge(turn_v, NT)
                    if s == 1 and c == 0:
                        pe.wait_ge(split, COPIES[("turn", NT - 1)] + 1)
                    free(BANK_BY, n, BANKS, bank_a, bank_v)
                    for d in range(DC):
                        last = three(bank[n % BANKS][:, 0:w], w16[:, d, 0, :], w16[:, d, 1, :],
                                     xT[:, d, 0, a:a + w], xT[:, d, 1, a:a + w], d == 0, d == DC - 1)
                    last.then_inc(bank_full, 1)
                elif o[0] == "q2":
                    s, c = o[1:]
                    n = TURN[o]
                    a, w = CHUNKS[c]
                    pe.wait_ge(q32, s * len(CHUNKS) + c + 1)
                    free(TURN_BY, n, TURNS, turn_a, turn_v)
                    nc.tensor.matmul(turn[n % TURNS][0:DA, 0:w], w2sb[DA:P, :], work[DA:P, a:a + w],
                                     start=True, stop=True).then_inc(turn_full, 1)
                elif o[0] == "logits":
                    s, t = o[1:]
                    n = LOGITS[o[1:]]
                    if t == 0:
                        pe.wait_ge(bank_v, reads(BANK_BY, BANK[("qk", s, len(CHUNKS) - 1)], "v"))
                        pe.wait_ge(turn_v, reads(TURN_BY, TURN[("q2", s, len(CHUNKS) - 1)], "v"))
                    if n:
                        pe.wait_ge(lg_exp, n)
                    for j, (a, w) in enumerate(CHUNKS):
                        last = three(lg[:, a:a + w], kq16[:, 2, t * P:(t + 1) * P], kq16[:, 3, t * P:(t + 1) * P],
                                     kq16[:, 0, a:a + w], kq16[:, 1, a:a + w], True, True)
                    last.then_inc(lg_full, 1)
                elif o[0] in ("into", "first", "carry", "base"):
                    t = o[1]
                    n = BANK[o]
                    if t == 0:
                        pe.wait_ge(u_lo, {"into": 1, "first": 2, "carry": 3, "base": 4}[o[0]])
                    u16 = {"into": ub16, "first": ua16, "carry": ua16, "base": ub16}[o[0]]
                    free(BANK_BY, n, BANKS, bank_a, bank_v)
                    r_ = rows(t)
                    for d in range(DC):
                        last = three(bank[n % BANKS][0:r_, :], xT[:, d, 0, t * P:t * P + r_], xT[:, d, 1, t * P:t * P + r_],
                                     u16[:, d, 0, :], u16[:, d, 1, :], d == 0, d == DC - 1)
                    last.then_inc(bank_full, 1)
                elif o[0] == "rowsum":
                    n = BANK[o]
                    pe.wait_ge(adj_lo, NT)
                    free(BANK_BY, n, BANKS, bank_a, bank_v)
                    for t in range(NT):
                        for kt in range(NT):
                            for half in range(2):
                                last = nc.tensor.matmul(bank[n % BANKS][0:rows(t), t:t + 1],
                                                        adj16[0:rows(kt), half, kt, t * P:t * P + rows(t)],
                                                        ones16[0:rows(kt), 0:1], start=(kt + half == 0),
                                                        stop=(kt == NT - 1 and half == 1))
                    last.then_inc(bank_full, 1)
                elif o[0] == "spread":
                    s, t = o[1:]
                    n = BANK[o]
                    if t == 0:
                        if s == 0:
                            pe.wait_ge(split, COPIES[("into", NT - 1)] + 1)
                        else:
                            pe.wait_ge(split, COPIES[("spread", 0, NT - 1, "sum")] + 1)
                    free(BANK_BY, n, BANKS, bank_a, bank_v)
                    src = rhs16 if s == 0 else mix16
                    r_ = rows(t)
                    for kt in range(NT):
                        k_ = rows(kt)
                        last = three(bank[n % BANKS][0:r_, :], adj16[0:k_, 0, kt, t * P:t * P + r_],
                                     adj16[0:k_, 1, kt, t * P:t * P + r_], src[0:k_, kt, 0, :], src[0:k_, kt, 1, :],
                                     kt == 0, kt == NT - 1)
                    last.then_inc(bank_full, 1)
                elif o[0] == "cut":
                    s, t = o[1:]
                    i = t % SLOTS
                    pe.wait_ge(a_ready, CUTS[o[1:]] + 1)
                    r_ = rows(t)
                    for b, blocks in enumerate(BLOCKS):
                        n = TURN[o + (b,)]
                        free(TURN_BY, n, TURNS, turn_a, turn_v)
                        for j, kt in enumerate(blocks):
                            last = nc.tensor.transpose(turn[n % TURNS][0:rows(kt), j * P:j * P + r_],
                                                       prob[0:r_, i, kt * P:kt * P + rows(kt)], ident[0:r_, 0:r_])
                        last.then_inc(turn_full, 1)
                elif o[0] == "attend":
                    s, t = o[1:]
                    n = BANK[o]
                    r = ATTENDS[o[1:]] % 2
                    pe.wait_ge(split, COPIES[("cut", s, t, len(BLOCKS) - 1)] + 1)
                    if t == 0:
                        if s == 0:
                            pe.wait_ge(hlo, NT)
                        else:
                            pe.wait_ge(split, COPIES[("carry", NT - 1)] + 1)
                    free(BANK_BY, n, BANKS, bank_a, bank_v)
                    src = feat16 if s == 0 else rhs16
                    r_ = rows(t)
                    for kt in range(NT):
                        k_ = rows(kt)
                        last = three(bank[n % BANKS][0:r_, :], attT[0:k_, r, 0, kt * P:kt * P + r_],
                                     attT[0:k_, r, 1, kt * P:kt * P + r_], src[0:k_, kt, 0, :], src[0:k_, kt, 1, :],
                                     kt == 0, kt == NT - 1)
                    last.then_inc(bank_full, 1)
                elif o[0] == "turn":
                    t = o[1]
                    n = TURN[o]
                    pe.wait_ge(xn_full, t + 1)
                    free(TURN_BY, n, TURNS, turn_a, turn_v)
                    r_ = rows(t)
                    for c in range(DC):
                        last = nc.tensor.transpose(turn[n % TURNS][:, c * P:c * P + r_], xnat[0:r_, c * P:(c + 1) * P],
                                                   ident[0:r_, 0:r_])
                    last.then_inc(turn_full, 1)


def kernel(**inputs):
    import numpy as np
    import concourse.bacc as bacc
    from concourse.bass_utils import run_bass_kernel_spmd as run

    nc = bacc.Bacc("TRN2", target_bir_lowering=False, num_devices=1, dynamic_dma_scratch_size=1024)
    names = ["x", "adj_t", "w1", "w2", "w3", "u10", "u11", "u20", "u21", "gamma", "beta"]
    src = {"x": "x", "w1": "L0_gnn_W1", "w2": "L0_gnn_W2", "w3": "L0_gnn_W3", "u10": "L0_gnn_U1_0",
           "u11": "L0_gnn_U1_1", "u20": "L0_gnn_U2_0", "u21": "L0_gnn_U2_1", "gamma": "L0_gnn_gamma",
           "beta": "L0_gnn_beta"}
    arrays, args = {}, []
    for n in names:
        a = np.ascontiguousarray(np.asarray(inputs["adj"]).T if n == "adj_t" else inputs[src[n]])
        arrays[n] = a
        args.append(nc.dram_tensor(n, a.shape, mybir.dt.from_np(a.dtype), kind="ExternalInput").ap())
    o = nc.dram_tensor("out", (N, D), FP32, kind="ExternalOutput").ap()
    graph_kernel(nc, *args, o)
    return run(nc, [arrays], core_ids=[0]).results[0]["out"]
```

```python
import concourse.bass as bass
from concourse import mybir
from contextlib import ExitStack

FP32 = mybir.dt.float32
FP16 = mybir.dt.float16
INT32 = mybir.dt.int32
ALU = mybir.AluOpType
ACT = mybir.ActivationFunctionType
AX = mybir.AxisListType

N, D, DA, P = 1354, 512, 64, 128
NT = -(-N // P)
DC = D // P
LN_EPS, P_TOP = 1e-5, 0.9
STEPS = 2
SLOTS = 4
GROUPS = [list(range(a, min(a + SLOTS, NT))) for a in range(0, NT, SLOTS)]
CHUNKS = [(c, min(512, N - c)) for c in range(0, N, 512)]
BLOCKS = [list(range(a, min(a + 4, NT))) for a in range(0, NT, 4)]

SC_X = 256.0
SC_U = 1024.0
SC_S = 128.0
SC_P = 4096.0
SC_K = 256.0

EVALS = [4, 6]
WINDOWS = [1, 2]
GUESS = (2.65, -2.76, 0.2)
OPEN = 16.0
HI0 = 1.5
LOG_BITS = 0.6931472 / 2 ** 23
LOG_ONE = 126.95 * 0.6931472
RSQRT_BITS = float(0x5F3759DF)
ROUND_INT = 12582912.0


def rows(t):
    return min(P, N - t * P)


def place(s, t):
    g = [g for g, group in enumerate(GROUPS) if t in group][0]
    i = t - GROUPS[g][0]
    return (1 if s == 1 and g == 1 else 0), i, (g % 2) * SLOTS + i


LN_HALVES = [list(range(0, 6)), list(range(6, NT))]
NORMS = [GROUPS[0], GROUPS[1], GROUPS[2]]

FILL = [
    [x for t in range(0, 3) for x in (("adj", t), ("into", t))] + [("weights", 1)]
    + [x for t in range(3, NT) for x in (("adj", t), ("into", t))]
    + [("first", t) for t in range(0, 3)] + [("rowsum",)],
    [("first", t) for t in range(3, NT)] + [("weights", 2)] + [("spread", 0, t) for t in range(0, 4)],
    [("spread", 0, t) for t in range(4, NT)],
]


def logits_bank(s, t):
    return t % 2 if t in GROUPS[0] or (s == 1 and t in GROUPS[1]) else 0


def search(s, g):
    return [("round", s, g, e) for e in range(EVALS[s])] + [("window", s, g, w) for w in range(WINDOWS[s])] \
        + [("found", s, g)]


def weave(main, extra):
    out = []
    for k in range(len(main) + 1):
        out += [x for pos, x in extra if pos == k]
        out += main[k:k + 1]
    return out


def schedule():
    yield ("prep",)
    for c in range(len(CHUNKS)):
        yield ("qk", 0, c)
    for c in range(len(CHUNKS)):
        yield ("q2", 0, c)
    for t in GROUPS[0]:
        yield ("logits", 0, t)
        if t == 1:
            yield ("weights", 0)
    for g, group in enumerate(GROUPS):
        if g == 1:
            yield ("invert",)
        yield ("guess", 0, g)
        yield from search(0, g)
        if g:
            yield ("attend", 0, group[0] - 1)
            yield ("turn", group[0] - 2)
        yield FILL[g][0]
        if g:
            yield ("turn", group[0] - 1)
        yield from FILL[g][1:]
        for t in group:
            yield ("cut", 0, t)
            if t > group[0] and t - 1 + SLOTS < NT:
                yield ("logits", 0, t - 1 + SLOTS)
            if t > group[0]:
                yield ("attend", 0, t - 1)
            if t > group[0] + 1:
                yield ("turn", t - 2)
        if group[-1] + SLOTS < NT:
            yield ("logits", 0, group[-1] + SLOTS)
    yield ("attend", 0, NT - 1)
    yield ("turn", NT - 2)
    for c in range(len(CHUNKS) - 1):
        yield ("qk", 1, c)
    yield ("turn", NT - 1)
    for c in range(len(CHUNKS) - 1):
        yield ("q2", 1, c)
    yield ("qk", 1, len(CHUNKS) - 1)
    yield ("q2", 1, len(CHUNKS) - 1)
    for t in GROUPS[0]:
        yield ("logits", 1, t)
    yield ("weights", 3)
    yield ("guess", 1, 0)
    for t in range(NT):
        yield ("carry", t)
    for t in range(NT):
        yield ("base", t)
    L = [("logits", 1, t) for t in GROUPS[1]]
    S = [("spread", 1, t) for t in range(NT)]
    yield from weave(search(1, 0), [(7, L[0]), (7, L[1]), (7, S[0]), (8, L[2]), (8, L[3]), (8, S[1])])
    for g in (0, 1):
        yield ("guess", 1, g + 1)
        for t in GROUPS[g]:
            yield ("cut", 1, t)
            if t > GROUPS[g][0]:
                yield ("attend", 1, t - 1)
        if g == 0:
            yield ("attend", 1, 3)
            yield from weave(search(1, 1), [(5, ("logits", 1, 8)), (5, S[2]), (6, ("logits", 1, 9)), (6, S[3]), (6, S[4]),
                                            (7, ("logits", 1, 10)), (7, S[5]), (7, S[6]), (7, S[7])])
        else:
            yield ("attend", 1, 7)
            yield from search(1, 2)
            for t in range(8, NT):
                yield S[t]
            yield ("norm", 0)
    for t in GROUPS[2]:
        yield ("cut", 1, t)
        if t > GROUPS[2][0]:
            yield ("attend", 1, t - 1)
    yield ("norm", 1)
    yield ("attend", 1, NT - 1)
    yield ("norm", 2)


ORDER = list(schedule())
BANK_READERS = {"qk": "av", "into": "a", "first": "a", "rowsum": "a", "spread": "a", "attend": "a", "carry": "a", "base": "a"}
TURN_READERS = {"ht": "av", "q2": "av", "cut": "a", "turn": "a"}


def bank_jobs():
    jobs = [o for o in ORDER if o[0] in BANK_READERS]
    return {o: n for n, o in enumerate(jobs)}, [BANK_READERS[o[0]] for o in jobs]


def turn_jobs():
    jobs = [("ht", t) for t in range(NT)]
    for o in ORDER:
        if o[0] == "cut":
            jobs += [o + (b,) for b in range(len(BLOCKS))]
        elif o[0] in ("q2", "turn"):
            jobs.append(o)
    return {o: n for n, o in enumerate(jobs)}, [TURN_READERS[o[0]] for o in jobs]


BANK, BANK_BY = bank_jobs()
TURN, TURN_BY = turn_jobs()
BANKS, TURNS = 2, 3


def reads(by, n, who):
    return sum(who in b for b in by[:n + 1])


COPIES = {}
for o in ORDER:
    if o[0] == "cut":
        for b in range(len(BLOCKS)):
            COPIES[o + (b,)] = len(COPIES)
    elif o[0] in ("into", "turn", "carry", "base", "spread") or o[:2] == ("attend", 1):
        COPIES[o] = len(COPIES)
        if o[0] == "spread" and o[1] == 0:
            COPIES[o + ("sum",)] = len(COPIES)
RING = 3
LOGITS = {o[1:]: n for n, o in enumerate(x for x in ORDER if x[0] == "logits")}
CUTS = {o[1:]: n for n, o in enumerate(x for x in ORDER if x[0] == "cut")}
ATTENDS = {o[1:]: n for n, o in enumerate(x for x in ORDER if x[0] == "attend")}


def graph_kernel(nc, x, adj_t, w1, w2, w3, u10, u11, u20, u21, gamma, beta, out):
    ctx = ExitStack()
    with ctx:
        def sb(name, shape, dt):
            return ctx.enter_context(nc.sbuf_tensor(name, shape, dt))

        def pb(name, shape, dt):
            return ctx.enter_context(nc.psum_tensor(name, shape, dt))

        def sem(name):
            return ctx.enter_context(nc.semaphore(name))

        adj16 = sb("adj16", [P, 2, NT, N], FP16)
        feat = sb("feat", [P, NT, D], FP32)
        feat16 = feat[:, :, :].bitcast(FP16).rearrange("p t (a d) -> p t a d", a=2)
        mix = sb("mix", [P, NT, D], FP32)
        mix16 = mix[:, :, :].bitcast(FP16).rearrange("p t (a d) -> p t a d", a=2)
        rhs = sb("rhs", [P, NT, D], FP32)
        rhs16 = rhs[:, :, :].bitcast(FP16).rearrange("p t (a d) -> p t a d", a=2)
        xT = sb("xT", [P, DC, 2, N], FP16)
        kq16 = sb("kq16", [DA, 4, NT * P], FP16)
        prob = sb("prob", [P, SLOTS, N], FP32)
        work = sb("work", [P, N], FP32)
        attT = sb("attT", [P, 2, 2, NT * P], FP16)
        w16 = sb("w16", [P, DC, 2, P], FP16)
        w2sb = sb("w2sb", [P, DA], FP32)
        ua16 = sb("ua16", [P, DC, 2, D], FP16)
        ub16 = attT[:, :, :, :].rearrange("p r a n -> p (r a n)")[:, 0:DC * 2 * D].rearrange(
            "p (c a d) -> p c a d", c=DC, a=2)
        ust = sb("ust", [P, DC, D], FP32)
        copy32 = sb("copy32", [P, RING, 512], FP32)
        xnat = sb("xnat", [P, D], FP32)
        ident = sb("ident", [P, P], FP32)
        ones16 = sb("ones16", [P, 2], FP16)
        stage = mix[:, :, :].rearrange("p t d -> p (t d)")[:, 0:4 * N].rearrange("p (r n) -> p r n", r=4)
        probs = [prob, xT[:, :, :, :].bitcast(FP32).rearrange("p c a n -> p (c a n)").rearrange("p (r n) -> p r n", r=SLOTS)]
        wst = prob[:, 0, 0:DC * P].rearrange("p (c n) -> p c n", c=DC)

        bst = sb("bst", [P, NT, 6], FP32)
        mv = sb("mv", [P, NT, 2], FP32)
        lnw = sb("lnw", [P, 5, NT], FP32)
        rinv = sb("rinv", [P, NT], FP32)
        mx = sb("mx", [P, 2 * SLOTS], FP32)
        nmx = sb("nmx", [P, 2, 2 * SLOTS], FP32)
        zz = sb("zz", [P, 2, 2 * SLOTS], FP32)
        zbits = zz[:, :, :].bitcast(INT32)
        tgt = sb("tgt", [P, SLOTS], FP32)
        tg = sb("tg", [P, 2, SLOTS], FP32)
        low = sb("low", [P, 2, SLOTS], FP32)
        high = sb("high", [P, 2, SLOTS], FP32)
        dif = sb("dif", [P, 2, SLOTS], FP32)
        sm = sb("sm", [P, 8, SLOTS], FP32)
        msk = sb("msk", [P, 2, SLOTS], INT32)
        top8 = sb("top8", [P, SLOTS, 8], FP32)
        pre8 = sb("pre8", [P, SLOTS, 8], FP32)
        wk8 = sb("wk8", [P, SLOTS, 8], FP32)
        eq8 = sb("eq8", [P, SLOTS, 8], FP32)
        next8 = eq8
        vcut = sb("vcut", [P, SLOTS], FP32)
        nvcut = sb("nvcut", [P, SLOTS], FP32)
        q1 = sb("q1", [P, SLOTS], FP32)
        zk = sb("zk", [P, SLOTS], FP32)
        rzs = sb("rzs", [P, NT], FP32)
        worst = [None]
        flag = sb("flag", [P, 32], FP32)
        flagT = sb("flagT", [P, 32], FP32)
        anyf = sb("anyf", [P, 1], FP32)
        any4 = sb("any4", [1, 4], FP32)
        anyi = sb("anyi", [1, 1], INT32)
        eq16 = work[:, :].bitcast(FP16)[:, 0:N]
        rk16 = work[:, :].bitcast(FP16)[:, N:2 * N]

        bank = [pb(f"bank{i}", [P, 512], FP32) for i in range(BANKS)]
        turns = pb("turns", [P, TURNS * 512], FP32)
        turn = [turns[:, i * 512:(i + 1) * 512] for i in range(TURNS)]
        lgs = [pb("lg", [P, 3 * 512], FP32), turns]

        s_x = [sem(f"s_x{i}") for i in range(len(LN_HALVES))]
        s_adj = [sem(f"s_adj{i}") for i in range(4)]
        s_w = sem("s_w")
        s_u = sem("s_u")
        s_fin = sem("s_fin")
        s_xr = sem("s_xr")
        s_out = sem("s_out")
        pool_c = sem("pool_c")
        dve = sem("dve")
        actn = sem("actn")
        pooln = sem("pooln")
        xpad = sem("xpad")
        adj_i = sem("adj_i")
        adj_hi = sem("adj_hi")
        adj_lo = sem("adj_lo")
        stats = sem("stats")
        h_ok = sem("h_ok")
        hhi = sem("hhi")
        hlo = sem("hlo")
        w_hi = sem("w_hi")
        w_lo = sem("w_lo")
        u_hi = sem("u_hi")
        u_lo = sem("u_lo")
        bank_full = sem("bank_full")
        bank_a = sem("bank_a")
        bank_v = sem("bank_v")
        turn_full = sem("turn_full")
        turn_a = sem("turn_a")
        turn_v = sem("turn_v")
        q32 = sem("q32")
        khi = sem("khi")
        copied = sem("copied")
        split = sem("split")
        xn_full = sem("xn_full")
        lg_full = sem("lg_full")
        lg_max = sem("lg_max")
        lg_exp = sem("lg_exp")
        gin = sem("gin")
        guess = sem("guess")
        a_ready = sem("a_ready")
        xb = sem("xb")
        o_ok = sem("o_ok")
        rs_one = sem("rs_one")
        rs_raw = sem("rs_raw")
        rs_ok = sem("rs_ok")

        block = ctx.enter_context(nc.Block())
        W_IN = [u11, u10, u21, u20]
        U_DST = [ub16, ua16, ua16, ub16]

        @block.sync
        def _(sp):
            m = LN_HALVES[1][0]
            sp.dma_start(rhs[:, 0:m, :], x[0:m * P, :].rearrange("(t p) d -> p t d", p=P)).then_inc(s_x[0], 16)
            sp.dma_start(rhs[:, m:NT - 1, :], x[m * P:(NT - 1) * P, :].rearrange("(t p) d -> p t d", p=P)).then_inc(s_x[1], 16)
            sp.wait_ge(xpad, 1)
            sp.dma_start(rhs[0:rows(NT - 1), NT - 1, :], x[(NT - 1) * P:N, :]).then_inc(s_x[1], 16)
            sp.dma_start(wst[:, :, 0:DA], w3.rearrange("(c p) n -> p c n", p=P)).then_inc(s_w, 16)
            sp.dma_start(wst[:, :, DA:P], w1.rearrange("(c p) n -> p c n", p=P)).then_inc(s_w, 16)
            sp.dma_start(w2sb[DA:P, :], w2[:, :]).then_inc(s_w, 16)
            for n in range(4):
                if n == 0:
                    sp.dma_start(ust[:, :, :], W_IN[0].rearrange("(c p) n -> p c n", p=P)).then_inc(s_u, 16)
                sp.dma_start(stage[0:rows(n), n, :], adj_t[n * P:n * P + rows(n), :]).then_inc(s_adj[n % 4], 16)
            def weights_load(n):
                sp.wait_ge(u_hi, n)
                sp.wait_ge(u_lo, n)
                sp.dma_start(ust[:, :, :], W_IN[n].rearrange("(c p) n -> p c n", p=P)).then_inc(s_u, 16)

            weights_load(1)
            for n in range(4, NT):
                sp.wait_ge(adj_lo, n - 3)
                sp.dma_start(stage[0:rows(n), n % 4, :], adj_t[n * P:n * P + rows(n), :]).then_inc(s_adj[n % 4], 16)
            weights_load(2)
            weights_load(3)
            sp.wait_ge(u_hi, 4)
            sp.wait_ge(u_lo, 4)
            sp.dma_start(ust[:, 2, :], gamma.rearrange("(a n) -> a n", a=1).broadcast_to((P, D))).then_inc(s_fin, 16)
            sp.dma_start(ust[:, 3, :], beta.rearrange("(a n) -> a n", a=1).broadcast_to((P, D))).then_inc(s_fin, 16)
            sp.wait_ge(bank_full, BANK[("spread", 1, NT - 1)] + 1)
            sp.dma_start(mix[:, 0:NT - 1, :], x[0:(NT - 1) * P, :].rearrange("(t p) d -> p t d", p=P)).then_inc(s_xr, 16)
            sp.dma_start(mix[0:rows(NT - 1), NT - 1, :], x[(NT - 1) * P:N, :]).then_inc(s_xr, 16)
            for t in range(NT):
                sp.wait_ge(o_ok, t + 1)
                sp.dma_start(out[t * P:t * P + rows(t), :], feat[0:rows(t), t, :]).then_inc(s_out, 16)
            sp.wait_ge(s_out, 16 * NT)

        @block.gpsimd
        def _(pool):
            steps = [0]

            def did(ins):
                steps[0] += 1
                ins.then_inc(pooln, 1)

            def settle():
                pool.wait_ge(pooln, steps[0])

            did(nc.gpsimd.memset(ident[:, :], 0.0))
            nc.gpsimd.memset(ones16[:, :], 1.0).then_inc(pool_c, 1)
            settle()
            nc.gpsimd.affine_select(out=ident[:, :], in_=ident[:, :], compare_op=ALU.not_equal, fill=1.0, base=0,
                                    pattern=[[-1, P]], channel_multiplier=1).then_inc(pool_c, 1)

            def lo_half(o, dst, hi, width):
                n = COPIES[o]
                pool.wait_ge(copied, n + 1)
                nc.gpsimd.tensor_tensor(out=dst, in0=copy32[:, n % RING, 0:width], in1=hi,
                                        op=ALU.subtract).then_inc(split, 1)

            def adj_identity(n):
                pool.wait_ge(s_adj[n % 4], 16 * (n // 4 + 1))
                a, r_ = n * P, rows(n)
                nc.gpsimd.tensor_tensor(out=stage[0:r_, n % 4, a:a + r_], in0=stage[0:r_, n % 4, a:a + r_],
                                        in1=ident[0:r_, 0:r_], op=ALU.add).then_inc(adj_i, 1)

            def weights_lo(n, dst):
                pool.wait_ge(u_hi, n + 1)
                for c in range(DC):
                    last = nc.gpsimd.tensor_tensor(out=dst[:, c, 1, :], in0=ust[:, c, :], in1=dst[:, c, 0, :],
                                                   op=ALU.subtract)
                last.then_inc(u_lo, 1)

            for o in ORDER:
                if o[0] == "prep":
                    pool.wait_ge(pool_c, 2)
                    for n in range(4):
                        adj_identity(n)
                elif o[0] == "adj":
                    n = o[1]
                    pool.wait_ge(adj_hi, n + 1)
                    nc.gpsimd.tensor_tensor(out=adj16[:, 1, n, :], in0=stage[:, n % 4, :], in1=adj16[:, 0, n, :],
                                            op=ALU.subtract).then_inc(adj_lo, 1)
                    if 0 <= n - 1 and n + 3 < NT:
                        adj_identity(n + 3)
                elif o[0] == "weights":
                    weights_lo(o[1], U_DST[o[1]])
                elif o[0] in ("into", "carry"):
                    lo_half(o, rhs16[:, o[1], 1, :], rhs16[:, o[1], 0, :], D)
                elif o[0] == "turn":
                    t = o[1]
                    n = COPIES[o]
                    pool.wait_ge(copied, n + 1)
                    nc.gpsimd.tensor_tensor(
                        out=xT[:, :, 1, t * P:t * P + rows(t)],
                        in0=copy32[:, n % RING, :].rearrange("p (c n) -> p c n", c=DC)[:, :, 0:rows(t)],
                        in1=xT[:, :, 0, t * P:t * P + rows(t)], op=ALU.subtract).then_inc(split, 1)
                elif o[0] == "cut":
                    r = CUTS[o[1:]] % 2
                    for b, blocks in enumerate(BLOCKS):
                        a, e = blocks[0] * P, (blocks[-1] + 1) * P
                        lo_half(o + (b,), attT[:, r, 1, a:e], attT[:, r, 0, a:e], e - a)
                elif o[0] == "spread" and o[1] == 0:
                    t = o[2]
                    n, m = COPIES[o], COPIES[o + ("sum",)]
                    pool.wait_ge(copied, n + 1)
                    if m >= RING:
                        pool.wait_ge(split, m - RING + 1)
                    did(nc.gpsimd.tensor_tensor(out=copy32[:, m % RING, :], in0=copy32[:, n % RING, :],
                                                in1=mix[:, t, :], op=ALU.add))
                    settle()
                    nc.gpsimd.sem_inc(split, 1)
                    lo_half(o + ("sum",), mix16[:, t, 1, :], mix16[:, t, 0, :], D)
                elif o[:2] in (("spread", 1), ("attend", 1)):
                    t = o[2]
                    n = COPIES[o]
                    before = max(m for m in (COPIES["base", t], COPIES["spread", 1, t], COPIES["attend", 1, t]) if m < n)
                    pool.wait_ge(split, before + 1)
                    pool.wait_ge(copied, n + 1)
                    nc.gpsimd.tensor_tensor(out=feat[:, t, :], in0=feat[:, t, :], in1=copy32[:, n % RING, :],
                                            op=ALU.add).then_inc(split, 1)
                elif o[0] == "base":
                    t = o[1]
                    n = COPIES[o]
                    pool.wait_ge(copied, n + 1)
                    did(nc.gpsimd.tensor_tensor(out=copy32[:, n % RING, :], in0=copy32[:, n % RING, :],
                                                in1=feat16[:, t, 0, :], op=ALU.add))
                    settle()
                    did(nc.gpsimd.tensor_tensor(out=copy32[:, n % RING, :], in0=copy32[:, n % RING, :],
                                                in1=feat16[:, t, 1, :], op=ALU.add))
                    settle()
                    nc.gpsimd.tensor_copy(feat[:, t, :], copy32[:, n % RING, :]).then_inc(split, 1)
                elif o[0] == "norm":
                    if o[1] == 0:
                        pool.wait_ge(s_fin, 32)
                        pool.wait_ge(s_xr, 32)
                        for t in range(NT):
                            r_ = rows(t)
                            nc.gpsimd.tensor_tensor(out=mix[0:r_, t, :], in0=mix[0:r_, t, :], in1=ust[0:r_, 3, :],
                                                    op=ALU.add).then_inc(xb, 1)

        @block.scalar
        def _(act):
            steps = [0]

            def did(ins):
                steps[0] += 1
                ins.then_inc(actn, 1)

            def settle():
                act.wait_ge(actn, steps[0])

            def hi_and_copy(o, src, scale, hi, cp, read):
                n = COPIES[o]
                if n >= RING:
                    act.wait_ge(split, n - RING + 1)
                nc.scalar.activation(hi, src, ACT.Copy, scale=scale).then_inc(actn, 1)
                steps[0] += 1
                did(nc.scalar.activation(cp, src, ACT.Copy, scale=scale))
                settle()
                nc.scalar.sem_inc(copied, 1)
                if read is not None:
                    nc.scalar.sem_inc(read, 1)

            def copy_only(o, src, scale, read):
                n = COPIES[o]
                if n >= RING:
                    act.wait_ge(split, n - RING + 1)
                did(nc.scalar.activation(copy32[:, n % RING, :], src, ACT.Copy, scale=scale))
                settle()
                nc.scalar.sem_inc(copied, 1)
                nc.scalar.sem_inc(read, 1)

            def weights_hi(n, dst):
                act.wait_ge(s_u, 16 * (n + 1))
                did(nc.scalar.activation(dst[:, :, 0, :], ust[:, :, :], ACT.Copy, scale=SC_U))
                settle()
                nc.scalar.activation(ust[:, :, :], ust[:, :, :], ACT.Copy, scale=SC_U).then_inc(u_hi, 1)

            for o in ORDER:
                if o[0] == "prep":
                    act.wait_ge(s_w, 48)
                    nc.scalar.activation(w16[:, :, 0, :], wst[:, :, :], ACT.Copy, scale=SC_U).then_inc(w_hi, 1)
                    for t in range(NT + 2):
                        if t < NT:
                            act.wait_ge(stats, 1 if t in LN_HALVES[0] else 2)
                            did(nc.scalar.activation(rhs[:, t, :], rhs[:, t, :], ACT.Relu, scale=lnw[:, 2, t:t + 1],
                                                     bias=lnw[:, 4, t:t + 1]))
                            settle()
                            nc.scalar.sem_inc(h_ok, 1)
                            nc.scalar.activation(feat16[:, t, 0, :], rhs[:, t, :], ACT.Copy, scale=SC_X).then_inc(hhi, 1)
                        if t >= 2:
                            u = t - 2
                            n = TURN[("ht", u)]
                            act.wait_ge(turn_full, n + 1)
                            nc.scalar.activation(xT[:, :, 0, u * P:u * P + rows(u)],
                                                 turn[n % TURNS][:, :].rearrange("p (c n) -> p c n", c=DC)[:, :, 0:rows(u)],
                                                 ACT.Copy, scale=SC_X).then_inc(turn_a, 1)
                elif o[0] == "adj":
                    n = o[1]
                    act.wait_ge(adj_i, n + 1)
                    did(nc.scalar.activation(adj16[:, 0, n, :], stage[:, n % 4, :], ACT.Copy, scale=SC_S))
                    settle()
                    nc.scalar.activation(stage[:, n % 4, :], stage[:, n % 4, :], ACT.Copy,
                                         scale=SC_S).then_inc(adj_hi, 1)
                elif o[0] == "weights":
                    if o[1] == 2:
                        act.wait_ge(bank_full, BANK[("first", NT - 1)] + 1)
                    elif o[1] == 3:
                        act.wait_ge(bank_full, BANK[("attend", 0, NT - 1)] + 1)
                    weights_hi(o[1], U_DST[o[1]])
                elif o[0] == "qk":
                    s, c = o[1:]
                    n = BANK[o]
                    a, w = CHUNKS[c]
                    act.wait_ge(bank_full, n + 1)
                    nc.scalar.activation(kq16[:, 0, a:a + w], bank[n % BANKS][0:DA, 0:w], ACT.Copy,
                                         scale=SC_K / (SC_X * SC_U)).then_inc(khi, 1)
                    did(nc.scalar.activation(work[DA:P, a:a + w], bank[n % BANKS][DA:P, 0:w], ACT.Copy,
                                             scale=1.0 / (SC_X * SC_U)))
                    settle()
                    nc.scalar.sem_inc(q32, 1)
                    nc.scalar.sem_inc(bank_a, 1)
                elif o[0] == "q2":
                    s, c = o[1:]
                    n = TURN[o]
                    a, w = CHUNKS[c]
                    act.wait_ge(turn_full, n + 1)
                    nc.scalar.activation(kq16[:, 2, a:a + w], turn[n % TURNS][0:DA, 0:w], ACT.Copy,
                                         scale=SC_K).then_inc(turn_a, 1)
                elif o[0] == "logits":
                    s, t = o[1:]
                    b, j, i = place(s, t)
                    n = LOGITS[o[1:]]
                    lg = lgs[logits_bank(s, t)]
                    act.wait_ge(lg_max, n + 1)
                    did(nc.scalar.activation(probs[b][:, j, :], lg[:, 0:N], ACT.Exp, scale=1.0 / SC_K ** 2,
                                             bias=nmx[:, 0, i:i + 1], accum_out=zz[:, 0, i:i + 1]))
                    settle()
                    did(nc.scalar.activation(lg[:, 0:N], lg[:, 0:N], ACT.Exp, scale=0.5 / SC_K ** 2,
                                             bias=nmx[:, 1, i:i + 1], accum_out=zz[:, 1, i:i + 1]))
                    settle()
                    nc.scalar.sem_inc(lg_exp, 1)
                elif o[0] == "guess":
                    s, g = o[1:]
                    k = len(GROUPS[g])
                    n = s * len(GROUPS) + g
                    act.wait_ge(gin, n + 1)
                    nc.scalar.activation(tg[:, 0, 0:k], sm[:, 0, 0:k], ACT.Exp).then_inc(guess, 1)
                elif o[0] in ("into", "carry"):
                    n = BANK[o]
                    if o == ("into", 0):
                        act.wait_ge(hlo, NT)
                    act.wait_ge(bank_full, n + 1)
                    hi_and_copy(o, bank[n % BANKS][:, :], 1.0 / SC_U, rhs16[:, o[1], 0, :],
                                copy32[:, COPIES[o] % RING, :], bank_a)
                elif o[0] == "first":
                    n = BANK[o]
                    if o[1] == 0:
                        act.wait_ge(adj_lo, NT)
                    act.wait_ge(bank_full, n + 1)
                    did(nc.scalar.activation(mix[:, o[1], :], bank[n % BANKS][:, :], ACT.Copy, scale=1.0 / SC_U))
                    settle()
                    nc.scalar.sem_inc(bank_a, 1)
                elif o[0] == "rowsum":
                    n = BANK[o]
                    r_ = rows(NT - 1)
                    act.wait_ge(rs_one, 1)
                    act.wait_ge(bank_full, n + 1)
                    did(nc.scalar.activation(rinv[:, 0:NT - 1], bank[n % BANKS][:, 0:NT - 1], ACT.Copy,
                                             scale=1.0 / SC_S))
                    did(nc.scalar.activation(rinv[0:r_, NT - 1:NT], bank[n % BANKS][0:r_, NT - 1:NT], ACT.Copy,
                                             scale=1.0 / SC_S))
                    settle()
                    nc.scalar.sem_inc(bank_a, 1)
                    nc.scalar.sem_inc(rs_raw, 1)
                elif o[0] == "base":
                    n = BANK[o]
                    act.wait_ge(bank_full, n + 1)
                    copy_only(o, bank[n % BANKS][:, :], 1.0 / SC_U, bank_a)
                elif o[0] == "spread":
                    s, t = o[1:]
                    n = BANK[o]
                    if s == 0 and t == 0:
                        act.wait_ge(rs_ok, 1)
                    act.wait_ge(bank_full, n + 1)
                    copy_only(o, bank[n % BANKS][:, :], rinv[:, t:t + 1], bank_a)
                    if s == 0:
                        m = COPIES[o + ("sum",)]
                        act.wait_ge(split, m)
                        did(nc.scalar.activation(mix16[:, t, 0, :], copy32[:, m % RING, :], ACT.Copy))
                        settle()
                        nc.scalar.sem_inc(copied, 1)
                elif o[0] == "cut":
                    s, t = o[1:]
                    r = CUTS[o[1:]] % 2
                    if s == 0 and t == 0:
                        act.wait_ge(bank_full, BANK[("into", NT - 1)] + 1)
                    if CUTS[o[1:]] >= 2:
                        k = CUTS[o[1:]] - 2
                        prev = ("attend", k // NT, k % NT)
                        act.wait_ge(bank_full, BANK[prev] + 1)
                    for b, blocks in enumerate(BLOCKS):
                        n = TURN[o + (b,)]
                        a, e = blocks[0] * P, (blocks[-1] + 1) * P
                        act.wait_ge(turn_full, n + 1)
                        hi_and_copy(o + (b,), turn[n % TURNS][:, 0:e - a], SC_P, attT[:, r, 0, a:e],
                                    copy32[:, COPIES[o + (b,)] % RING, 0:e - a], turn_a)
                elif o[:2] == ("attend", 1):
                    act.wait_ge(bank_full, BANK[o] + 1)
                    copy_only(o, bank[BANK[o] % BANKS][:, :], rzs[:, o[2]:o[2] + 1], bank_a)
                elif o[0] == "attend":
                    s, t = o[1:]
                    n = BANK[o]
                    act.wait_ge(bank_full, n + 1)
                    if t > 0:
                        act.wait_ge(turn_full, TURN[("turn", t - 1)] + 1)
                    did(nc.scalar.activation(xnat[:, :], bank[n % BANKS][:, :], ACT.Copy, scale=rzs[:, t:t + 1]))
                    settle()
                    nc.scalar.sem_inc(xn_full, 1)
                    nc.scalar.sem_inc(bank_a, 1)
                elif o[0] == "turn":
                    t = o[1]
                    n = TURN[o]
                    act.wait_ge(turn_full, n + 1)
                    src = turn[n % TURNS][:, :].rearrange("p (c n) -> p c n", c=DC)[:, :, 0:rows(t)]
                    cp = copy32[:, COPIES[o] % RING, :].rearrange("p (c n) -> p c n", c=DC)[:, :, 0:rows(t)]
                    hi_and_copy(o, src, SC_X, xT[:, :, 0, t * P:t * P + rows(t)], cp, turn_a)

        @block.vector
        def _(v):
            steps = [0]

            def did(ins):
                steps[0] += 1
                return ins.then_inc(dve, 1)

            def settle():
                v.wait_ge(dve, steps[0])

            def step(ins):
                did(ins)
                settle()

            def rsqrt(y, r, w):
                step(nc.vector.tensor_scalar(r.bitcast(INT32), y.bitcast(INT32), -0.5, RSQRT_BITS, ALU.mult, ALU.add))
                for _ in range(3):
                    step(nc.vector.tensor_tensor(w, r, r, ALU.mult))
                    step(nc.vector.tensor_tensor(w, w, y, ALU.mult))
                    step(nc.vector.tensor_scalar(w, w, -0.5, 1.5, ALU.mult, ALU.add))
                    step(nc.vector.tensor_tensor(r, r, w, ALU.mult))

            halves = [work[:, :].bitcast(FP16)[:, h * N:(h + 1) * N] for h in range(2)]

            def mass(p, i, cut, dst, scratch=work[:, :]):
                return nc.vector.scalar_tensor_tensor(out=scratch, in0=p[:, i, :], scalar=cut, in1=p[:, i, :],
                                                      op0=ALU.is_ge, op1=ALU.mult, accum_out=dst)

            def below(p, i, bound, dst=None):
                return nc.vector.scalar_tensor_tensor(out=work[:, :], in0=p[:, i, :], scalar=bound, in1=p[:, i, :],
                                                      op0=ALU.is_lt, op1=ALU.mult, accum_out=dst)

            def window(p, i, fence):
                fence(below(p, i, high[:, 0, i:i + 1]))
                fence(nc.vector.max(top8[:, i, :], work[:, :]))
                fence(mass(p, i, top8[:, i, 7:8], tg[:, 1, i:i + 1]))

            def upper_bound_moves(k, fence):
                K = slice(0, k)
                fence(nc.vector.tensor_tensor(msk[:, 0, K], tg[:, 1, K], tgt[:, K], ALU.is_lt))
                fence(nc.vector.tensor_copy(tg[:, 0, K], top8[:, K, 7]))
                fence(nc.vector.copy_predicated(high[:, :, K], msk[:, 0:1, K].broadcast_to((P, 2, k)), tg[:, :, K]))

            def cuts(k, go, fence):
                K = slice(0, k)
                for i in range(k):
                    go(nc.vector.tensor_tensor_scan(pre8[:, i, :], top8[:, i, :], top8[:, i, :],
                                                    high[:, 1, i:i + 1], ALU.add, ALU.max))
                fence(nc.vector.tensor_tensor(sm[:, 5, K], tg[:, 1, K], tgt[:, K], ALU.is_lt))
                tgt8 = tgt[:, K].rearrange("p (k a) -> p k a", a=1).broadcast_to((P, k, 8))
                go(nc.vector.tensor_tensor(sm[:, 4, K], tg[:, 1, K], pre8[:, K, 7], ALU.subtract))
                fence(nc.vector.tensor_tensor(wk8[:, K, :], pre8[:, K, :], tgt8, ALU.is_ge))
                fence(nc.vector.tensor_tensor(wk8[:, K, :], wk8[:, K, :], top8[:, K, :], ALU.mult))
                fence(nc.vector.tensor_reduce(vcut[:, K], wk8[:, K, :], AX.X, ALU.max))
                fence(nc.vector.tensor_tensor(vcut[:, K], vcut[:, K], top8[:, K, 7], ALU.max))
                v8 = vcut[:, K].rearrange("p (k a) -> p k a", a=1).broadcast_to((P, k, 8))
                go(nc.vector.reciprocal(sm[:, 2, K], vcut[:, K]))
                go(nc.vector.tensor_scalar(nvcut[:, K], vcut[:, K], -1.0, None, ALU.mult))
                go(nc.vector.tensor_tensor(wk8[:, K, :], top8[:, K, :], v8, ALU.is_gt))
                fence(nc.vector.tensor_tensor(eq8[:, K, :], top8[:, K, :], v8, ALU.is_equal))
                go(nc.vector.tensor_tensor(wk8[:, K, :], wk8[:, K, :], top8[:, K, :], ALU.mult))
                go(nc.vector.tensor_reduce(sm[:, 3, K], eq8[:, K, :], AX.X, ALU.add))
                fence(nc.vector.tensor_tensor(sm[:, 4, K], sm[:, 4, K], sm[:, 2, K], ALU.mult))
                go(nc.vector.tensor_reduce(sm[:, 0, K], wk8[:, K, :], AX.X, ALU.add))
                fence(nc.vector.tensor_tensor(sm[:, 4, K], sm[:, 4, K], eq8[:, K, 7], ALU.mult))
                go(nc.vector.tensor_tensor(sm[:, 3, K], sm[:, 3, K], sm[:, 4, K], ALU.add))
                fence(nc.vector.tensor_tensor(sm[:, 0, K], sm[:, 0, K], high[:, 1, K], ALU.add))
                go(nc.vector.tensor_scalar(sm[:, 3, K], sm[:, 3, K], ROUND_INT, -ROUND_INT, ALU.add, ALU.add))
                fence(nc.vector.tensor_tensor(sm[:, 1, K], tgt[:, K], sm[:, 0, K], ALU.subtract))
                fence(nc.vector.tensor_tensor(sm[:, 1, K], sm[:, 1, K], sm[:, 2, K], ALU.mult))
                fence(nc.vector.tensor_scalar(q1[:, K], sm[:, 1, K], 0.5, 1.0, ALU.max, ALU.add))
                fence(nc.vector.tensor_tensor(sm[:, 3, K], sm[:, 3, K], q1[:, K], ALU.is_ge))
                fence(nc.vector.scalar_tensor_tensor(out=sm[:, 3, K], in0=sm[:, 5, K], scalar=OPEN, in1=sm[:, 3, K],
                                                     op0=ALU.mult, op1=ALU.add))
                fence(nc.vector.tensor_reduce(flag[:, 0:1], sm[:, 3, K], AX.X, ALU.max))
                fence(nc.vector.transpose(flagT[:, :], flag[:, :]))
                fence(nc.vector.tensor_reduce(anyf[:, 0:1], flagT[:, :], AX.X, ALU.max))
                for q in range(4):
                    (fence if q == 3 else go)(nc.vector.tensor_copy(any4[0:1, q:q + 1], anyf[32 * q:32 * q + 1, 0:1]))
                fence(nc.vector.tensor_reduce(anyi[0:1, 0:1], any4[0:1, :], AX.X, ALU.max))

            nc.vector.memset(rhs[64:P, NT - 1, :], 0.0).then_inc(xpad, 1)
            v.wait_ge(xpad, 1)
            for half, tiles in enumerate(LN_HALVES):
                a, e = tiles[0], tiles[-1] + 1
                v.wait_ge(s_x[half], 16 * (1 + half))
                for t in tiles:
                    did(nc.vector.bn_stats(bst[:, t, :], rhs[:, t, :]))
                settle()
                for t in tiles:
                    did(nc.vector.bn_aggr(mv[:, t, :], bst[:, t, :]))
                settle()
                step(nc.vector.tensor_scalar(lnw[:, 0, a:e], mv[:, a:e, 1], LN_EPS, None, ALU.add))
                rsqrt(lnw[:, 0, a:e], lnw[:, 2, a:e], lnw[:, 3, a:e])
                step(nc.vector.scalar_tensor_tensor(out=lnw[:, 4, a:e], in0=mv[:, a:e, 0], scalar=-1.0,
                                                    in1=lnw[:, 2, a:e], op0=ALU.mult, op1=ALU.mult))
                nc.vector.sem_inc(stats, 1)
            v.wait_ge(s_w, 48)
            v.wait_ge(w_hi, 1)
            nc.vector.scalar_tensor_tensor(out=w16[:, :, 1, :], in0=wst[:, :, :], scalar=SC_U, in1=w16[:, :, 0, :],
                                           op0=ALU.mult, op1=ALU.subtract).then_inc(w_lo, 1)
            nc.vector.memset(rinv[:, :], 1.0).then_inc(rs_one, 1)
            step(nc.vector.memset(flag[:, :], 0.0))
            step(nc.vector.memset(anyf[:, :], 0.0))
            for t in range(NT):
                v.wait_ge(hhi, t + 1)
                nc.vector.scalar_tensor_tensor(out=feat16[:, t, 1, :], in0=rhs[:, t, :], scalar=SC_X,
                                               in1=feat16[:, t, 0, :], op0=ALU.mult, op1=ALU.subtract).then_inc(hlo, 1)
                n = TURN[("ht", t)]
                v.wait_ge(turn_a, n + 1)
                nc.vector.scalar_tensor_tensor(out=xT[:, :, 1, t * P:t * P + rows(t)],
                                               in0=turn[n % TURNS][:, :].rearrange("p (c n) -> p c n", c=DC)[:, :, 0:rows(t)],
                                               scalar=SC_X, in1=xT[:, :, 0, t * P:t * P + rows(t)],
                                               op0=ALU.mult, op1=ALU.subtract).then_inc(turn_v, 1)
            for o in ORDER:
                if o[0] == "qk":
                    s, c = o[1:]
                    n = BANK[o]
                    a, w = CHUNKS[c]
                    v.wait_ge(khi, s * len(CHUNKS) + c + 1)
                    nc.vector.scalar_tensor_tensor(out=kq16[:, 1, a:a + w], in0=bank[n % BANKS][0:DA, 0:w],
                                                   scalar=SC_K / (SC_X * SC_U), in1=kq16[:, 0, a:a + w],
                                                   op0=ALU.mult, op1=ALU.subtract).then_inc(bank_v, 1)
                elif o[0] == "q2":
                    s, c = o[1:]
                    n = TURN[o]
                    a, w = CHUNKS[c]
                    v.wait_ge(turn_a, n + 1)
                    lo = nc.vector.scalar_tensor_tensor(out=kq16[:, 3, a:a + w], in0=turn[n % TURNS][0:DA, 0:w],
                                                        scalar=SC_K, in1=kq16[:, 2, a:a + w],
                                                        op0=ALU.mult, op1=ALU.subtract)
                    if c == len(CHUNKS) - 1:
                        step(lo)
                        pad = NT * P - N
                        lo = nc.vector.tensor_copy(kq16[:, 2:4, N:N + pad], kq16[:, 2:4, N - pad:N])
                    lo.then_inc(turn_v, 1)
                elif o[0] == "invert":
                    v.wait_ge(rs_raw, 1)
                    step(nc.vector.tensor_scalar(rinv[:, :], rinv[:, :], 1e-12, None, ALU.max))
                    step(nc.vector.reciprocal(rinv[:, :], rinv[:, :]))
                    step(nc.vector.tensor_scalar(rinv[:, :], rinv[:, :], 1.0 / SC_S, None, ALU.mult))
                    nc.vector.sem_inc(rs_ok, 1)
                elif o[0] == "logits":
                    s, t = o[1:]
                    i = place(s, t)[2]
                    n = LOGITS[o[1:]]
                    lg = lgs[logits_bank(s, t)]
                    v.wait_ge(lg_full, n + 1)
                    step(nc.vector.reduce_max(mx[:, i:i + 1], lg[:, 0:N], AX.X))
                    did(nc.vector.tensor_scalar(nmx[:, 0, i:i + 1], mx[:, i:i + 1], -1.0 / SC_K ** 2, None, ALU.mult))
                    did(nc.vector.tensor_scalar(nmx[:, 1, i:i + 1], mx[:, i:i + 1], -0.5 / SC_K ** 2, None, ALU.mult))
                    settle()
                    nc.vector.sem_inc(lg_max, 1)
                elif o[0] == "guess":
                    s, g = o[1:]
                    group = GROUPS[g]
                    k = len(group)
                    K = slice(0, k)
                    Z = slice((g % 2) * SLOTS, (g % 2) * SLOTS + k)
                    ng = s * len(GROUPS) + g
                    v.wait_ge(lg_exp, s * NT + group[-1] + 1)
                    step(nc.vector.tensor_scalar(sm[:, 1, K], zbits[:, 0, Z], GUESS[0] * LOG_BITS,
                                                 GUESS[2] - (GUESS[0] + GUESS[1]) * LOG_ONE, ALU.mult, ALU.add))
                    step(nc.vector.scalar_tensor_tensor(out=sm[:, 0, K], in0=zbits[:, 1, Z], scalar=GUESS[1] * LOG_BITS,
                                                        in1=sm[:, 1, K],
                                                        op0=ALU.mult, op1=ALU.add))
                    nc.vector.sem_inc(gin, 1)
                    did(nc.vector.tensor_scalar(tgt[:, K], zz[:, 0, Z], P_TOP, None, ALU.mult))
                    did(nc.vector.memset(high[:, 0, K], HI0))
                    did(nc.vector.memset(high[:, 1, K], 0.0))
                    did(nc.vector.memset(low[:, 0, K], 0.0))
                    did(nc.vector.tensor_copy(low[:, 1, K], zz[:, 0, Z]))
                    v.wait_ge(guess, ng + 1)
                    step(nc.vector.tensor_scalar(tg[:, 0, K], tg[:, 0, K], 1.0, None, ALU.min))
                elif o[0] == "round":
                    s, g, e = o[1:]
                    k = len(GROUPS[g])
                    K = slice(0, k)
                    p = probs[place(s, GROUPS[g][0])[0]]
                    for i in range(k):
                        if i >= 2:
                            v.wait_ge(dve, steps[0] - 1)
                        did(mass(p, i, tg[:, 0, i:i + 1], tg[:, 1, i:i + 1], halves[i % 2]))
                    settle()
                    did(nc.vector.tensor_tensor(msk[:, 0, K], tg[:, 1, K], tgt[:, K], ALU.is_ge))
                    step(nc.vector.tensor_tensor(msk[:, 1, K], tg[:, 1, K], tgt[:, K], ALU.is_lt))
                    did(nc.vector.copy_predicated(low[:, :, K], msk[:, 0:1, K].broadcast_to((P, 2, k)), tg[:, :, K]))
                    step(nc.vector.copy_predicated(high[:, :, K], msk[:, 1:2, K].broadcast_to((P, 2, k)), tg[:, :, K]))
                    if e == EVALS[s] - 1:
                        continue
                    did(nc.vector.tensor_tensor(dif[:, :, K], high[:, :, K], low[:, :, K], ALU.subtract))
                    step(nc.vector.tensor_tensor(sm[:, 1, K], low[:, 1, K], tgt[:, K], ALU.subtract))
                    did(nc.vector.reciprocal(sm[:, 0, K], dif[:, 1, K]))
                    step(nc.vector.scalar_tensor_tensor(out=sm[:, 1, K], in0=low[:, 0, K], scalar=4.0, in1=sm[:, 1, K],
                                                        op0=ALU.mult, op1=ALU.add))
                    step(nc.vector.scalar_tensor_tensor(out=sm[:, 1, K], in0=sm[:, 1, K], scalar=-1.0, in1=sm[:, 0, K],
                                                        op0=ALU.mult, op1=ALU.mult))
                    step(nc.vector.tensor_scalar(sm[:, 1, K], sm[:, 1, K], 0.02, 0.98, ALU.max, ALU.min))
                    step(nc.vector.tensor_tensor(sm[:, 1, K], sm[:, 1, K], dif[:, 0, K], ALU.mult))
                    step(nc.vector.tensor_tensor(tg[:, 0, K], sm[:, 1, K], low[:, 0, K], ALU.add))
                elif o[0] == "window":
                    s, g, w = o[1:]
                    k = len(GROUPS[g])
                    p = probs[place(s, GROUPS[g][0])[0]]
                    K = slice(0, k)
                    Z = slice((g % 2) * SLOTS, (g % 2) * SLOTS + k)
                    if w == 0:
                        for i in range(k):
                            step(below(p, i, high[:, 0, i:i + 1]))
                            step(nc.vector.max(top8[:, i, :], work[:, :]))
                    else:
                        for i in range(k):
                            step(below(p, i, top8[:, i, 7:8], sm[:, 6, i:i + 1]))
                            step(nc.vector.max(next8[:, i, :], work[:, :]))
                        did(nc.vector.tensor_copy(tg[:, 0, K], top8[:, K, 7]))
                        step(nc.vector.tensor_tensor(tg[:, 1, K], zz[:, 0, Z], sm[:, 6, K], ALU.subtract))
                        step(nc.vector.tensor_tensor(msk[:, 0, K], tg[:, 1, K], tgt[:, K], ALU.is_lt))
                        did(nc.vector.copy_predicated(high[:, :, K], msk[:, 0:1, K].broadcast_to((P, 2, k)), tg[:, :, K]))
                        step(nc.vector.copy_predicated(top8[:, K, :], msk[:, 0, K].rearrange("p (k a) -> p k a", a=1)
                                                       .broadcast_to((P, k, 8)), next8[:, K, :]))
                    if w == WINDOWS[s] - 1:
                        for i in range(k):
                            if i >= 2:
                                v.wait_ge(dve, steps[0] - 1)
                            did(mass(p, i, top8[:, i, 7:8], tg[:, 1, i:i + 1], halves[i % 2]))
                        settle()
                elif o[0] == "found":
                    s, g = o[1:]
                    k = len(GROUPS[g])
                    p = probs[place(s, GROUPS[g][0])[0]]
                    cuts(k, did, step)

                    def some_row_is_open():
                        worst[0] = v.value_load(anyi[0:1, 0:1], min_val=0, max_val=int(OPEN) + 1)
                        return worst[0] >= int(OPEN)

                    def fence(ins):
                        nc.vector.drain()

                    with v.While(some_row_is_open):
                        upper_bound_moves(k, fence)
                        for i in range(k):
                            window(p, i, fence)
                        cuts(k, fence, fence)
                elif o[0] == "cut":
                    s, t = o[1:]
                    b, i = place(s, t)[:2]
                    p = probs[b]
                    step(nc.vector.scalar_tensor_tensor(out=p[:, i, :], in0=p[:, i, :], scalar=vcut[:, i:i + 1],
                                                        in1=p[:, i, :], op0=ALU.is_ge, op1=ALU.mult,
                                                        accum_out=zk[:, i:i + 1]))
                    with v.If(worst[0] > 0):
                        nc.vector.tensor_scalar(eq16, p[:, i, :], vcut[:, i:i + 1], None, ALU.is_equal)
                        nc.vector.drain()
                        nc.vector.tensor_tensor_scan(rk16, eq16, eq16, 0.0, ALU.add, ALU.max)
                        nc.vector.drain()
                        nc.vector.scalar_tensor_tensor(out=eq16, in0=rk16, scalar=q1[:, i:i + 1], in1=eq16,
                                                       op0=ALU.is_ge, op1=ALU.mult)
                        nc.vector.drain()
                        nc.vector.scalar_tensor_tensor(out=p[:, i, :], in0=eq16, scalar=nvcut[:, i:i + 1],
                                                       in1=p[:, i, :], op0=ALU.mult, op1=ALU.add,
                                                       accum_out=zk[:, i:i + 1])
                        nc.vector.drain()
                    did(nc.vector.reciprocal(rzs[:, t:t + 1], zk[:, i:i + 1]))
                    settle()
                    step(nc.vector.tensor_scalar(rzs[:, t:t + 1], rzs[:, t:t + 1],
                                                 1.0 / (SC_P * SC_X) if s == 0 else 1.0 / SC_P, None, ALU.mult))
                    nc.vector.sem_inc(a_ready, 1)
                elif o[0] == "norm":
                    tiles = NORMS[o[1]]
                    a, e = tiles[0], tiles[-1] + 1
                    v.wait_ge(split, max(COPIES[kind, 1, t] for kind in ("spread", "attend") for t in tiles) + 1)
                    for t in tiles:
                        did(nc.vector.bn_stats(bst[:, t, :], feat[:, t, :]))
                    settle()
                    for t in tiles:
                        did(nc.vector.bn_aggr(mv[:, t, :], bst[:, t, :]))
                    settle()
                    step(nc.vector.tensor_scalar(lnw[:, 0, a:e], mv[:, a:e, 1], LN_EPS * SC_X ** 2, None, ALU.add))
                    rsqrt(lnw[:, 0, a:e], lnw[:, 2, a:e], lnw[:, 3, a:e])
                    v.wait_ge(s_fin, 32)
                    for t in tiles:
                        r_ = rows(t)
                        did(nc.vector.scalar_tensor_tensor(out=feat[0:r_, t, :], in0=feat[0:r_, t, :],
                                                           scalar=mv[0:r_, t, 0:1], in1=ust[0:r_, 2, :],
                                                           op0=ALU.subtract, op1=ALU.mult))
                    for k, t in enumerate(tiles):
                        r_ = rows(t)
                        v.wait_ge(dve, steps[0] - (len(tiles) - 1 - k))
                        v.wait_ge(xb, t + 1)
                        nc.vector.scalar_tensor_tensor(out=feat[0:r_, t, :], in0=feat[0:r_, t, :],
                                                       scalar=lnw[0:r_, 2, t:t + 1], in1=mix[0:r_, t, :],
                                                       op0=ALU.mult, op1=ALU.add).then_inc(o_ok, 1)

        @block.tensor
        def _(pe):
            def three(dst, l_hi, l_lo, r_hi, r_lo, first, last):
                nc.tensor.matmul(dst, l_hi, r_hi, start=first, stop=False)
                nc.tensor.matmul(dst, l_hi, r_lo, start=False, stop=False)
                return nc.tensor.matmul(dst, l_lo, r_hi, start=False, stop=last)

            def free(jobs_by, n, ring, sem_a, sem_v):
                if n >= ring:
                    for who, sm_ in (("a", sem_a), ("v", sem_v)):
                        if who in jobs_by[n - ring]:
                            pe.wait_ge(sm_, reads(jobs_by, n - ring, who))

            pe.wait_ge(pool_c, 2)
            for t in range(NT):
                n = TURN[("ht", t)]
                pe.wait_ge(h_ok, t + 1)
                free(TURN_BY, n, TURNS, turn_a, turn_v)
                r_ = rows(t)
                for c in range(DC):
                    last = nc.tensor.transpose(turn[n % TURNS][:, c * P:c * P + r_], rhs[0:r_, t, c * P:(c + 1) * P],
                                               ident[0:r_, 0:r_])
                last.then_inc(turn_full, 1)

            for o in ORDER:
                if o[0] == "qk":
                    s, c = o[1:]
                    n = BANK[o]
                    a, w = CHUNKS[c]
                    if s == 0 and c == 0:
                        pe.wait_ge(w_lo, 1)
                        pe.wait_ge(turn_v, NT)
                    if s == 1:
                        pe.wait_ge(split, COPIES[("turn", (a + w - 1) // P)] + 1)
                    free(BANK_BY, n, BANKS, bank_a, bank_v)
                    for d in range(DC):
                        last = three(bank[n % BANKS][:, 0:w], w16[:, d, 0, :], w16[:, d, 1, :],
                                     xT[:, d, 0, a:a + w], xT[:, d, 1, a:a + w], d == 0, d == DC - 1)
                    last.then_inc(bank_full, 1)
                elif o[0] == "q2":
                    s, c = o[1:]
                    n = TURN[o]
                    a, w = CHUNKS[c]
                    pe.wait_ge(q32, s * len(CHUNKS) + c + 1)
                    free(TURN_BY, n, TURNS, turn_a, turn_v)
                    nc.tensor.matmul(turn[n % TURNS][0:DA, 0:w], w2sb[DA:P, :], work[DA:P, a:a + w],
                                     start=True, stop=True).then_inc(turn_full, 1)
                elif o[0] == "logits":
                    s, t = o[1:]
                    n = LOGITS[o[1:]]
                    if t == 0:
                        pe.wait_ge(bank_v, reads(BANK_BY, BANK[("qk", s, len(CHUNKS) - 1)], "v"))
                        pe.wait_ge(turn_v, reads(TURN_BY, TURN[("q2", s, len(CHUNKS) - 1)], "v"))
                    lg = lgs[logits_bank(s, t)]
                    if t == 1:
                        last = TURN[("q2", s, len(CHUNKS) - 1)]
                        pe.wait_ge(turn_a, reads(TURN_BY, last, "a"))
                        pe.wait_ge(turn_v, reads(TURN_BY, last, "v"))
                    elif t in (2, 3) or (s == 1 and t in GROUPS[1]):
                        pe.wait_ge(lg_exp, n - 1)
                    elif n:
                        pe.wait_ge(lg_exp, n)
                    for j, (a, w) in enumerate(CHUNKS):
                        last = three(lg[:, a:a + w], kq16[:, 2, t * P:(t + 1) * P], kq16[:, 3, t * P:(t + 1) * P],
                                     kq16[:, 0, a:a + w], kq16[:, 1, a:a + w], True, True)
                    last.then_inc(lg_full, 1)
                elif o[0] in ("into", "first", "carry", "base"):
                    t = o[1]
                    n = BANK[o]
                    if t == 0:
                        pe.wait_ge(u_lo, {"into": 1, "first": 2, "carry": 3, "base": 4}[o[0]])
                    u16 = {"into": ub16, "first": ua16, "carry": ua16, "base": ub16}[o[0]]
                    free(BANK_BY, n, BANKS, bank_a, bank_v)
                    r_ = rows(t)
                    for d in range(DC):
                        last = three(bank[n % BANKS][0:r_, :], xT[:, d, 0, t * P:t * P + r_], xT[:, d, 1, t * P:t * P + r_],
                                     u16[:, d, 0, :], u16[:, d, 1, :], d == 0, d == DC - 1)
                    last.then_inc(bank_full, 1)
                elif o[0] == "rowsum":
                    n = BANK[o]
                    pe.wait_ge(adj_lo, NT)
                    free(BANK_BY, n, BANKS, bank_a, bank_v)
                    for t in range(NT):
                        for kt in range(NT):
                            for half in range(2):
                                last = nc.tensor.matmul(bank[n % BANKS][0:rows(t), t:t + 1],
                                                        adj16[0:rows(kt), half, kt, t * P:t * P + rows(t)],
                                                        ones16[0:rows(kt), 0:1], start=(kt + half == 0),
                                                        stop=(kt == NT - 1 and half == 1))
                    last.then_inc(bank_full, 1)
                elif o[0] == "spread":
                    s, t = o[1:]
                    n = BANK[o]
                    if t == 0:
                        if s == 0:
                            pe.wait_ge(split, COPIES[("into", NT - 1)] + 1)
                        else:
                            pe.wait_ge(split, COPIES[("spread", 0, NT - 1, "sum")] + 1)
                    free(BANK_BY, n, BANKS, bank_a, bank_v)
                    src = rhs16 if s == 0 else mix16
                    r_ = rows(t)
                    for kt in range(NT):
                        k_ = rows(kt)
                        last = three(bank[n % BANKS][0:r_, :], adj16[0:k_, 0, kt, t * P:t * P + r_],
                                     adj16[0:k_, 1, kt, t * P:t * P + r_], src[0:k_, kt, 0, :], src[0:k_, kt, 1, :],
                                     kt == 0, kt == NT - 1)
                    last.then_inc(bank_full, 1)
                elif o[0] == "cut":
                    s, t = o[1:]
                    b, i = place(s, t)[:2]
                    p = probs[b]
                    pe.wait_ge(a_ready, CUTS[o[1:]] + 1)
                    r_ = rows(t)
                    for h, blocks in enumerate(BLOCKS):
                        n = TURN[o + (h,)]
                        free(TURN_BY, n, TURNS, turn_a, turn_v)
                        for j, kt in enumerate(blocks):
                            last = nc.tensor.transpose(turn[n % TURNS][0:rows(kt), j * P:j * P + r_],
                                                       p[0:r_, i, kt * P:kt * P + rows(kt)], ident[0:r_, 0:r_])
                        last.then_inc(turn_full, 1)
                elif o[0] == "attend":
                    s, t = o[1:]
                    n = BANK[o]
                    r = ATTENDS[o[1:]] % 2
                    pe.wait_ge(split, COPIES[("cut", s, t, len(BLOCKS) - 1)] + 1)
                    if t == 0:
                        if s == 0:
                            pe.wait_ge(hlo, NT)
                        else:
                            pe.wait_ge(split, COPIES[("carry", NT - 1)] + 1)
                    free(BANK_BY, n, BANKS, bank_a, bank_v)
                    src = feat16 if s == 0 else rhs16
                    r_ = rows(t)
                    for kt in range(NT):
                        k_ = rows(kt)
                        last = three(bank[n % BANKS][0:r_, :], attT[0:k_, r, 0, kt * P:kt * P + r_],
                                     attT[0:k_, r, 1, kt * P:kt * P + r_], src[0:k_, kt, 0, :], src[0:k_, kt, 1, :],
                                     kt == 0, kt == NT - 1)
                    last.then_inc(bank_full, 1)
                elif o[0] == "turn":
                    t = o[1]
                    n = TURN[o]
                    pe.wait_ge(xn_full, t + 1)
                    free(TURN_BY, n, TURNS, turn_a, turn_v)
                    r_ = rows(t)
                    for c in range(DC):
                        last = nc.tensor.transpose(turn[n % TURNS][:, c * P:c * P + r_], xnat[0:r_, c * P:(c + 1) * P],
                                                   ident[0:r_, 0:r_])
                    last.then_inc(turn_full, 1)


def kernel(**inputs):
    import numpy as np
    import concourse.bacc as bacc
    from concourse.bass_utils import run_bass_kernel_spmd as run

    nc = bacc.Bacc("TRN2", target_bir_lowering=False, num_devices=1, dynamic_dma_scratch_size=1024)
    names = ["x", "adj_t", "w1", "w2", "w3", "u10", "u11", "u20", "u21", "gamma", "beta"]
    src = {"x": "x", "w1": "L0_gnn_W1", "w2": "L0_gnn_W2", "w3": "L0_gnn_W3", "u10": "L0_gnn_U1_0",
           "u11": "L0_gnn_U1_1", "u20": "L0_gnn_U2_0", "u21": "L0_gnn_U2_1", "gamma": "L0_gnn_gamma",
           "beta": "L0_gnn_beta"}
    arrays, args = {}, []
    for n in names:
        a = np.ascontiguousarray(np.asarray(inputs["adj"]).T if n == "adj_t" else inputs[src[n]])
        arrays[n] = a
        args.append(nc.dram_tensor(n, a.shape, mybir.dt.from_np(a.dtype), kind="ExternalInput").ap())
    o = nc.dram_tensor("out", (N, D), FP32, kind="ExternalOutput").ap()
    graph_kernel(nc, *args, o)
    return run(nc, [arrays], core_ids=[0]).results[0]["out"]
```

```python
import concourse.bass as bass
from concourse import mybir
from contextlib import ExitStack

FP32 = mybir.dt.float32
FP16 = mybir.dt.float16
INT32 = mybir.dt.int32
ALU = mybir.AluOpType
ACT = mybir.ActivationFunctionType
AX = mybir.AxisListType

N, D, DA, P = 1354, 512, 64, 128
NT = -(-N // P)
DC = D // P
LN_EPS, P_TOP = 1e-5, 0.9
STEPS = 2
SLOTS = 4
GROUPS = [list(range(a, min(a + SLOTS, NT))) for a in range(0, NT, SLOTS)]
CHUNKS = [(c, min(512, N - c)) for c in range(0, N, 512)]
BLOCKS = [list(range(a, min(a + 4, NT))) for a in range(0, NT, 4)]

SC_X = 256.0
SC_U = 1024.0
SC_S = 128.0
SC_P = 4096.0
SC_K = 256.0

EVALS = [4, 6]
WINDOWS = [1, 2]
GUESS = (2.65, -2.76, 0.2)
OPEN = 16.0
HI0 = 1.5
LOG_BITS = 0.6931472 / 2 ** 23
LOG_ONE = 126.95 * 0.6931472
RSQRT_BITS = float(0x5F3759DF)
ROUND_INT = 12582912.0


def rows(t):
    return min(P, N - t * P)


def place(s, t):
    g = [g for g, group in enumerate(GROUPS) if t in group][0]
    i = t - GROUPS[g][0]
    return (1 if s == 1 and g == 1 else 0), i, (g % 2) * SLOTS + i


LN_HALVES = [list(range(0, 6)), list(range(6, NT))]
NORMS = [GROUPS[0], GROUPS[1], GROUPS[2][:-1], GROUPS[2][-1:]]

FILL = [
    [x for t in range(0, 3) for x in (("adj", t), ("into", t))] + [("weights", 1)]
    + [x for t in range(3, NT) for x in (("adj", t), ("into", t))]
    + [("first", t) for t in range(0, 3)] + [("rowsum",)],
    [("first", t) for t in range(3, NT)] + [("weights", 2)] + [("spread", 0, t) for t in range(0, 4)],
    [("spread", 0, t) for t in range(4, NT)],
]


def logits_bank(s, t):
    return t % 2 if t in GROUPS[0] or (s == 1 and t in GROUPS[1]) else 0


def search(s, g):
    return [("round", s, g, e) for e in range(EVALS[s])] + [("window", s, g, w) for w in range(WINDOWS[s])] \
        + [("found", s, g)]


def weave(main, extra):
    out = []
    for k in range(len(main) + 1):
        out += [x for pos, x in extra if pos == k]
        out += main[k:k + 1]
    return out


def schedule():
    yield ("prep",)
    for c in range(len(CHUNKS)):
        yield ("qk", 0, c)
    for c in range(len(CHUNKS)):
        yield ("q2", 0, c)
    for t in GROUPS[0]:
        yield ("logits", 0, t)
        if t == 1:
            yield ("weights", 0)
    for g, group in enumerate(GROUPS):
        if g == 1:
            yield ("invert",)
        yield ("guess", 0, g)
        yield from search(0, g)
        if g:
            yield ("attend", 0, group[0] - 1)
            yield ("turn", group[0] - 2)
        yield FILL[g][0]
        if g:
            yield ("turn", group[0] - 1)
        yield from FILL[g][1:]
        for t in group:
            yield ("cut", 0, t)
            if t > group[0] and t - 1 + SLOTS < NT:
                yield ("logits", 0, t - 1 + SLOTS)
            if t > group[0]:
                yield ("attend", 0, t - 1)
            if t > group[0] + 1:
                yield ("turn", t - 2)
        if group[-1] + SLOTS < NT:
            yield ("logits", 0, group[-1] + SLOTS)
    yield ("attend", 0, NT - 1)
    yield ("turn", NT - 2)
    for c in range(len(CHUNKS) - 1):
        yield ("qk", 1, c)
    yield ("turn", NT - 1)
    for c in range(len(CHUNKS) - 1):
        yield ("q2", 1, c)
    yield ("qk", 1, len(CHUNKS) - 1)
    yield ("q2", 1, len(CHUNKS) - 1)
    for t in GROUPS[0]:
        yield ("logits", 1, t)
    yield ("weights", 3)
    yield ("guess", 1, 0)
    for t in range(NT):
        yield ("carry", t)
    for t in range(NT):
        yield ("base", t)
    L = [("logits", 1, t) for t in GROUPS[1]]
    S = [("spread", 1, t) for t in range(NT)]
    yield from weave(search(1, 0), [(7, L[0]), (7, L[1]), (7, S[0]), (8, L[2]), (8, L[3]), (8, S[1])])
    for g in (0, 1):
        yield ("guess", 1, g + 1)
        for t in GROUPS[g]:
            yield ("cut", 1, t)
            if t > GROUPS[g][0]:
                yield ("attend", 1, t - 1)
        if g == 0:
            yield ("attend", 1, 3)
            yield from weave(search(1, 1), [(5, ("logits", 1, 8)), (5, S[2]), (6, ("logits", 1, 9)), (6, S[3]), (6, S[4]),
                                            (7, ("logits", 1, 10)), (7, S[5]), (7, S[6]), (7, S[7])])
        else:
            yield ("attend", 1, 7)
            yield from search(1, 2)
            for t in range(8, NT):
                yield S[t]
            yield ("norm", 0)
    for t in GROUPS[2]:
        yield ("cut", 1, t)
        if t > GROUPS[2][0]:
            yield ("attend", 1, t - 1)
    yield ("norm", 1)
    yield ("norm", 2)
    yield ("attend", 1, NT - 1)
    yield ("norm", 3)


ORDER = list(schedule())
BANK_READERS = {"qk": "av", "into": "a", "first": "a", "rowsum": "a", "spread": "a", "attend": "a", "carry": "a", "base": "a"}
TURN_READERS = {"ht": "av", "q2": "av", "cut": "a", "turn": "a"}


def bank_jobs():
    jobs = [o for o in ORDER if o[0] in BANK_READERS]
    return {o: n for n, o in enumerate(jobs)}, [BANK_READERS[o[0]] for o in jobs]


def turn_jobs():
    jobs = [("ht", t) for t in range(NT)]
    for o in ORDER:
        if o[0] == "cut":
            jobs += [o + (b,) for b in range(len(BLOCKS))]
        elif o[0] in ("q2", "turn"):
            jobs.append(o)
    return {o: n for n, o in enumerate(jobs)}, [TURN_READERS[o[0]] for o in jobs]


BANK, BANK_BY = bank_jobs()
TURN, TURN_BY = turn_jobs()
BANKS, TURNS = 2, 3


def reads(by, n, who):
    return sum(who in b for b in by[:n + 1])


COPIES = {}
for o in ORDER:
    if o[0] == "cut":
        for b in range(len(BLOCKS)):
            COPIES[o + (b,)] = len(COPIES)
    elif o[0] in ("into", "turn", "carry", "base", "spread") or o[:2] == ("attend", 1):
        COPIES[o] = len(COPIES)
        if o[0] == "spread" and o[1] == 0:
            COPIES[o + ("sum",)] = len(COPIES)
RING = 3
LOGITS = {o[1:]: n for n, o in enumerate(x for x in ORDER if x[0] == "logits")}
CUTS = {o[1:]: n for n, o in enumerate(x for x in ORDER if x[0] == "cut")}
ATTENDS = {o[1:]: n for n, o in enumerate(x for x in ORDER if x[0] == "attend")}


def graph_kernel(nc, x, adj_t, w1, w2, w3, u10, u11, u20, u21, gamma, beta, out):
    ctx = ExitStack()
    with ctx:
        def sb(name, shape, dt):
            return ctx.enter_context(nc.sbuf_tensor(name, shape, dt))

        def pb(name, shape, dt):
            return ctx.enter_context(nc.psum_tensor(name, shape, dt))

        def sem(name):
            return ctx.enter_context(nc.semaphore(name))

        adj16 = sb("adj16", [P, 2, NT, N], FP16)
        feat = sb("feat", [P, NT, D], FP32)
        feat16 = feat[:, :, :].bitcast(FP16).rearrange("p t (a d) -> p t a d", a=2)
        mix = sb("mix", [P, NT, D], FP32)
        mix16 = mix[:, :, :].bitcast(FP16).rearrange("p t (a d) -> p t a d", a=2)
        rhs = sb("rhs", [P, NT, D], FP32)
        rhs16 = rhs[:, :, :].bitcast(FP16).rearrange("p t (a d) -> p t a d", a=2)
        xT = sb("xT", [P, DC, 2, N], FP16)
        kq16 = sb("kq16", [DA, 4, NT * P], FP16)
        prob = sb("prob", [P, SLOTS, N], FP32)
        work = sb("work", [P, N], FP32)
        attT = sb("attT", [P, 2, 2, NT * P], FP16)
        w16 = sb("w16", [P, DC, 2, P], FP16)
        w2sb = sb("w2sb", [P, DA], FP32)
        ua16 = sb("ua16", [P, DC, 2, D], FP16)
        ub16 = attT[:, :, :, :].rearrange("p r a n -> p (r a n)")[:, 0:DC * 2 * D].rearrange(
            "p (c a d) -> p c a d", c=DC, a=2)
        ust = sb("ust", [P, DC, D], FP32)
        copy32 = sb("copy32", [P, RING, 512], FP32)
        xnat = sb("xnat", [P, D], FP32)
        ident = sb("ident", [P, P], FP32)
        ones16 = sb("ones16", [P, 2], FP16)
        stage = mix[:, :, :].rearrange("p t d -> p (t d)")[:, 0:4 * N].rearrange("p (r n) -> p r n", r=4)
        probs = [prob, xT[:, :, :, :].bitcast(FP32).rearrange("p c a n -> p (c a n)").rearrange("p (r n) -> p r n", r=SLOTS)]
        wst = prob[:, 0, 0:DC * P].rearrange("p (c n) -> p c n", c=DC)

        bst = sb("bst", [P, NT, 6], FP32)
        mv = sb("mv", [P, NT, 2], FP32)
        lnw = sb("lnw", [P, 5, NT], FP32)
        rinv = sb("rinv", [P, NT], FP32)
        mx = sb("mx", [P, 2 * SLOTS], FP32)
        nmx = sb("nmx", [P, 2, 2 * SLOTS], FP32)
        zz = sb("zz", [P, 2, 2 * SLOTS], FP32)
        zbits = zz[:, :, :].bitcast(INT32)
        tgt = sb("tgt", [P, SLOTS], FP32)
        tg = sb("tg", [P, 2, SLOTS], FP32)
        low = sb("low", [P, 2, SLOTS], FP32)
        high = sb("high", [P, 2, SLOTS], FP32)
        dif = sb("dif", [P, 2, SLOTS], FP32)
        sm = sb("sm", [P, 8, SLOTS], FP32)
        msk = sb("msk", [P, 2, SLOTS], INT32)
        top8 = sb("top8", [P, SLOTS, 8], FP32)
        pre8 = sb("pre8", [P, SLOTS, 8], FP32)
        wk8 = sb("wk8", [P, SLOTS, 8], FP32)
        eq8 = sb("eq8", [P, SLOTS, 8], FP32)
        next8 = eq8
        vcut = sb("vcut", [P, SLOTS], FP32)
        q1 = sb("q1", [P, SLOTS], FP32)
        zk = sb("zk", [P, SLOTS], FP32)
        rzs = sb("rzs", [P, NT], FP32)
        worst = [None]
        flag = sb("flag", [P, 32], FP32)
        flagT = sb("flagT", [P, 32], FP32)
        anyf = sb("anyf", [P, 1], FP32)
        any4 = sb("any4", [1, 4], FP32)
        anyi = sb("anyi", [1, 1], INT32)
        side = work[:, :].bitcast(mybir.dt.bfloat16)[:, 0:N]
        rk16 = work[:, :].bitcast(FP16)[:, N:2 * N]

        bank = [pb(f"bank{i}", [P, 512], FP32) for i in range(BANKS)]
        turns = pb("turns", [P, TURNS * 512], FP32)
        turn = [turns[:, i * 512:(i + 1) * 512] for i in range(TURNS)]
        lgs = [pb("lg", [P, 3 * 512], FP32), turns]

        x_loaded = [sem(f"x_loaded{i}") for i in range(len(LN_HALVES))]
        adj_loaded = [sem(f"adj_loaded{i}") for i in range(4)]
        w_loaded = sem("w_loaded")
        u_loaded = sem("u_loaded")
        gamma_beta_loaded = sem("gamma_beta_loaded")
        x_reloaded = sem("x_reloaded")
        out_stored = sem("out_stored")
        constants_ready = sem("constants_ready")
        vector_steps = sem("vector_steps")
        scalar_steps = sem("scalar_steps")
        gpsimd_steps = sem("gpsimd_steps")
        x_padded = sem("x_padded")
        identity_added = sem("identity_added")
        adj_hi = sem("adj_hi")
        adj_lo = sem("adj_lo")
        stats = sem("stats")
        h_ready = sem("h_ready")
        h_hi = sem("h_hi")
        h_lo = sem("h_lo")
        w_hi = sem("w_hi")
        w_lo = sem("w_lo")
        u_hi = sem("u_hi")
        u_lo = sem("u_lo")
        bank_full = sem("bank_full")
        bank_read_scalar = sem("bank_read_scalar")
        bank_read_vector = sem("bank_read_vector")
        turn_full = sem("turn_full")
        turn_read_scalar = sem("turn_read_scalar")
        turn_read_vector = sem("turn_read_vector")
        q_ready = sem("q_ready")
        k_hi = sem("k_hi")
        copied = sem("copied")
        split = sem("split")
        xa_ready = sem("xa_ready")
        logits_ready = sem("logits_ready")
        max_ready = sem("max_ready")
        exp_ready = sem("exp_ready")
        guess_input = sem("guess_input")
        guess = sem("guess")
        kept_ready = sem("kept_ready")
        residual_ready = sem("residual_ready")
        out_ready = sem("out_ready")
        rowsum_ones = sem("rowsum_ones")
        rowsum_ready = sem("rowsum_ready")
        rowsum_inverted = sem("rowsum_inverted")

        block = ctx.enter_context(nc.Block())
        W_IN = [u11, u10, u21, u20]
        U_DST = [ub16, ua16, ua16, ub16]

        @block.sync
        def _(sp):
            m = LN_HALVES[1][0]
            sp.dma_start(rhs[:, 0:m, :], x[0:m * P, :].rearrange("(t p) d -> p t d", p=P)).then_inc(x_loaded[0], 16)
            sp.dma_start(rhs[:, m:NT - 1, :], x[m * P:(NT - 1) * P, :].rearrange("(t p) d -> p t d", p=P)).then_inc(x_loaded[1], 16)
            sp.wait_ge(x_padded, 1)
            sp.dma_start(rhs[0:rows(NT - 1), NT - 1, :], x[(NT - 1) * P:N, :]).then_inc(x_loaded[1], 16)
            sp.dma_start(wst[:, :, 0:DA], w3.rearrange("(c p) n -> p c n", p=P)).then_inc(w_loaded, 16)
            sp.dma_start(wst[:, :, DA:P], w1.rearrange("(c p) n -> p c n", p=P)).then_inc(w_loaded, 16)
            sp.dma_start(w2sb[DA:P, :], w2[:, :]).then_inc(w_loaded, 16)
            for n in range(4):
                if n == 0:
                    sp.dma_start(ust[:, :, :], W_IN[0].rearrange("(c p) n -> p c n", p=P)).then_inc(u_loaded, 16)
                sp.dma_start(stage[0:rows(n), n, :], adj_t[n * P:n * P + rows(n), :]).then_inc(adj_loaded[n % 4], 16)
            def weights_load(n):
                sp.wait_ge(u_hi, n)
                sp.wait_ge(u_lo, n)
                sp.dma_start(ust[:, :, :], W_IN[n].rearrange("(c p) n -> p c n", p=P)).then_inc(u_loaded, 16)

            weights_load(1)
            for n in range(4, NT):
                sp.wait_ge(adj_lo, n - 3)
                sp.dma_start(stage[0:rows(n), n % 4, :], adj_t[n * P:n * P + rows(n), :]).then_inc(adj_loaded[n % 4], 16)
            weights_load(2)
            weights_load(3)
            sp.wait_ge(u_hi, 4)
            sp.wait_ge(u_lo, 4)
            sp.dma_start(ust[:, 2, :], gamma.rearrange("(a n) -> a n", a=1).broadcast_to((P, D))).then_inc(gamma_beta_loaded, 16)
            sp.dma_start(ust[:, 3, :], beta.rearrange("(a n) -> a n", a=1).broadcast_to((P, D))).then_inc(gamma_beta_loaded, 16)
            sp.wait_ge(bank_full, BANK[("spread", 1, NT - 1)] + 1)
            sp.dma_start(mix[:, 0:NT - 1, :], x[0:(NT - 1) * P, :].rearrange("(t p) d -> p t d", p=P)).then_inc(x_reloaded, 16)
            sp.dma_start(mix[0:rows(NT - 1), NT - 1, :], x[(NT - 1) * P:N, :]).then_inc(x_reloaded, 16)
            for t in range(NT):
                sp.wait_ge(out_ready, t + 1)
                sp.dma_start(out[t * P:t * P + rows(t), :], feat[0:rows(t), t, :]).then_inc(out_stored, 16)
            sp.wait_ge(out_stored, 16 * NT)

        @block.gpsimd
        def _(pool):
            steps = [0]

            def did(ins):
                steps[0] += 1
                ins.then_inc(gpsimd_steps, 1)

            def settle():
                pool.wait_ge(gpsimd_steps, steps[0])

            did(nc.gpsimd.memset(ident[:, :], 0.0))
            nc.gpsimd.memset(ones16[:, :], 1.0).then_inc(constants_ready, 1)
            settle()
            nc.gpsimd.affine_select(out=ident[:, :], in_=ident[:, :], compare_op=ALU.not_equal, fill=1.0, base=0,
                                    pattern=[[-1, P]], channel_multiplier=1).then_inc(constants_ready, 1)

            def lo_half(o, dst, hi, width):
                n = COPIES[o]
                pool.wait_ge(copied, n + 1)
                nc.gpsimd.tensor_tensor(out=dst, in0=copy32[:, n % RING, 0:width], in1=hi,
                                        op=ALU.subtract).then_inc(split, 1)

            def adj_identity(n):
                pool.wait_ge(adj_loaded[n % 4], 16 * (n // 4 + 1))
                a, r_ = n * P, rows(n)
                nc.gpsimd.tensor_tensor(out=stage[0:r_, n % 4, a:a + r_], in0=stage[0:r_, n % 4, a:a + r_],
                                        in1=ident[0:r_, 0:r_], op=ALU.add).then_inc(identity_added, 1)

            def weights_lo(n, dst):
                pool.wait_ge(u_hi, n + 1)
                for c in range(DC):
                    last = nc.gpsimd.tensor_tensor(out=dst[:, c, 1, :], in0=ust[:, c, :], in1=dst[:, c, 0, :],
                                                   op=ALU.subtract)
                last.then_inc(u_lo, 1)

            for o in ORDER:
                if o[0] == "prep":
                    pool.wait_ge(constants_ready, 2)
                    for n in range(4):
                        adj_identity(n)
                elif o[0] == "adj":
                    n = o[1]
                    pool.wait_ge(adj_hi, n + 1)
                    nc.gpsimd.tensor_tensor(out=adj16[:, 1, n, :], in0=stage[:, n % 4, :], in1=adj16[:, 0, n, :],
                                            op=ALU.subtract).then_inc(adj_lo, 1)
                    if 0 <= n - 1 and n + 3 < NT:
                        adj_identity(n + 3)
                elif o[0] == "weights":
                    weights_lo(o[1], U_DST[o[1]])
                elif o[0] in ("into", "carry"):
                    lo_half(o, rhs16[:, o[1], 1, :], rhs16[:, o[1], 0, :], D)
                elif o[0] == "turn":
                    t = o[1]
                    n = COPIES[o]
                    pool.wait_ge(copied, n + 1)
                    nc.gpsimd.tensor_tensor(
                        out=xT[:, :, 1, t * P:t * P + rows(t)],
                        in0=copy32[:, n % RING, :].rearrange("p (c n) -> p c n", c=DC)[:, :, 0:rows(t)],
                        in1=xT[:, :, 0, t * P:t * P + rows(t)], op=ALU.subtract).then_inc(split, 1)
                elif o[0] == "cut":
                    r = CUTS[o[1:]] % 2
                    for b, blocks in enumerate(BLOCKS):
                        a, e = blocks[0] * P, (blocks[-1] + 1) * P
                        lo_half(o + (b,), attT[:, r, 1, a:e], attT[:, r, 0, a:e], e - a)
                elif o[0] == "spread" and o[1] == 0:
                    t = o[2]
                    n, m = COPIES[o], COPIES[o + ("sum",)]
                    pool.wait_ge(copied, n + 1)
                    if m >= RING:
                        pool.wait_ge(split, m - RING + 1)
                    did(nc.gpsimd.tensor_tensor(out=copy32[:, m % RING, :], in0=copy32[:, n % RING, :],
                                                in1=mix[:, t, :], op=ALU.add))
                    settle()
                    nc.gpsimd.sem_inc(split, 1)
                    lo_half(o + ("sum",), mix16[:, t, 1, :], mix16[:, t, 0, :], D)
                elif o[:2] in (("spread", 1), ("attend", 1)):
                    t = o[2]
                    n = COPIES[o]
                    before = max(m for m in (COPIES["base", t], COPIES["spread", 1, t], COPIES["attend", 1, t]) if m < n)
                    pool.wait_ge(split, before + 1)
                    pool.wait_ge(copied, n + 1)
                    nc.gpsimd.tensor_tensor(out=feat[:, t, :], in0=feat[:, t, :], in1=copy32[:, n % RING, :],
                                            op=ALU.add).then_inc(split, 1)
                elif o[0] == "base":
                    t = o[1]
                    n = COPIES[o]
                    pool.wait_ge(copied, n + 1)
                    did(nc.gpsimd.tensor_tensor(out=copy32[:, n % RING, :], in0=copy32[:, n % RING, :],
                                                in1=feat16[:, t, 0, :], op=ALU.add))
                    settle()
                    did(nc.gpsimd.tensor_tensor(out=copy32[:, n % RING, :], in0=copy32[:, n % RING, :],
                                                in1=feat16[:, t, 1, :], op=ALU.add))
                    settle()
                    nc.gpsimd.tensor_copy(feat[:, t, :], copy32[:, n % RING, :]).then_inc(split, 1)
                elif o[0] == "norm":
                    if o[1] == 0:
                        pool.wait_ge(gamma_beta_loaded, 32)
                        pool.wait_ge(x_reloaded, 32)
                        for t in range(NT):
                            r_ = rows(t)
                            nc.gpsimd.tensor_tensor(out=mix[0:r_, t, :], in0=mix[0:r_, t, :], in1=ust[0:r_, 3, :],
                                                    op=ALU.add).then_inc(residual_ready, 1)

        @block.scalar
        def _(act):
            steps = [0]

            def did(ins):
                steps[0] += 1
                ins.then_inc(scalar_steps, 1)

            def settle():
                act.wait_ge(scalar_steps, steps[0])

            def hi_and_copy(o, src, scale, hi, cp, reader):
                n = COPIES[o]
                if n >= RING:
                    act.wait_ge(split, n - RING + 1)
                nc.scalar.activation(hi, src, ACT.Copy, scale=scale).then_inc(scalar_steps, 1)
                steps[0] += 1
                did(nc.scalar.activation(cp, src, ACT.Copy, scale=scale))
                settle()
                nc.scalar.sem_inc(copied, 1)
                if reader is not None:
                    nc.scalar.sem_inc(reader, 1)

            def copy_only(o, src, scale, read):
                n = COPIES[o]
                if n >= RING:
                    act.wait_ge(split, n - RING + 1)
                did(nc.scalar.activation(copy32[:, n % RING, :], src, ACT.Copy, scale=scale))
                settle()
                nc.scalar.sem_inc(copied, 1)
                nc.scalar.sem_inc(read, 1)

            def weights_hi(n, dst):
                act.wait_ge(u_loaded, 16 * (n + 1))
                did(nc.scalar.activation(dst[:, :, 0, :], ust[:, :, :], ACT.Copy, scale=SC_U))
                settle()
                nc.scalar.activation(ust[:, :, :], ust[:, :, :], ACT.Copy, scale=SC_U).then_inc(u_hi, 1)

            for o in ORDER:
                if o[0] == "prep":
                    act.wait_ge(w_loaded, 48)
                    nc.scalar.activation(w16[:, :, 0, :], wst[:, :, :], ACT.Copy, scale=SC_U).then_inc(w_hi, 1)
                    for t in range(NT + 2):
                        if t < NT:
                            act.wait_ge(stats, 1 if t in LN_HALVES[0] else 2)
                            did(nc.scalar.activation(rhs[:, t, :], rhs[:, t, :], ACT.Relu, scale=lnw[:, 2, t:t + 1],
                                                     bias=lnw[:, 4, t:t + 1]))
                            settle()
                            nc.scalar.sem_inc(h_ready, 1)
                            nc.scalar.activation(feat16[:, t, 0, :], rhs[:, t, :], ACT.Copy, scale=SC_X).then_inc(h_hi, 1)
                        if t >= 2:
                            u = t - 2
                            n = TURN[("ht", u)]
                            act.wait_ge(turn_full, n + 1)
                            nc.scalar.activation(xT[:, :, 0, u * P:u * P + rows(u)],
                                                 turn[n % TURNS][:, :].rearrange("p (c n) -> p c n", c=DC)[:, :, 0:rows(u)],
                                                 ACT.Copy, scale=SC_X).then_inc(turn_read_scalar, 1)
                elif o[0] == "adj":
                    n = o[1]
                    act.wait_ge(identity_added, n + 1)
                    did(nc.scalar.activation(adj16[:, 0, n, :], stage[:, n % 4, :], ACT.Copy, scale=SC_S))
                    settle()
                    nc.scalar.activation(stage[:, n % 4, :], stage[:, n % 4, :], ACT.Copy,
                                         scale=SC_S).then_inc(adj_hi, 1)
                elif o[0] == "weights":
                    if o[1] == 2:
                        act.wait_ge(bank_full, BANK[("first", NT - 1)] + 1)
                    elif o[1] == 3:
                        act.wait_ge(bank_full, BANK[("attend", 0, NT - 1)] + 1)
                    weights_hi(o[1], U_DST[o[1]])
                elif o[0] == "qk":
                    s, c = o[1:]
                    n = BANK[o]
                    a, w = CHUNKS[c]
                    act.wait_ge(bank_full, n + 1)
                    nc.scalar.activation(kq16[:, 0, a:a + w], bank[n % BANKS][0:DA, 0:w], ACT.Copy,
                                         scale=SC_K / (SC_X * SC_U)).then_inc(k_hi, 1)
                    did(nc.scalar.activation(work[DA:P, a:a + w], bank[n % BANKS][DA:P, 0:w], ACT.Copy,
                                             scale=1.0 / (SC_X * SC_U)))
                    settle()
                    nc.scalar.sem_inc(q_ready, 1)
                    nc.scalar.sem_inc(bank_read_scalar, 1)
                elif o[0] == "q2":
                    s, c = o[1:]
                    n = TURN[o]
                    a, w = CHUNKS[c]
                    act.wait_ge(turn_full, n + 1)
                    nc.scalar.activation(kq16[:, 2, a:a + w], turn[n % TURNS][0:DA, 0:w], ACT.Copy,
                                         scale=SC_K).then_inc(turn_read_scalar, 1)
                elif o[0] == "logits":
                    s, t = o[1:]
                    b, j, i = place(s, t)
                    n = LOGITS[o[1:]]
                    lg = lgs[logits_bank(s, t)]
                    act.wait_ge(max_ready, n + 1)
                    did(nc.scalar.activation(probs[b][:, j, :], lg[:, 0:N], ACT.Exp, scale=1.0 / SC_K ** 2,
                                             bias=nmx[:, 0, i:i + 1], accum_out=zz[:, 0, i:i + 1]))
                    settle()
                    did(nc.scalar.activation(lg[:, 0:N], lg[:, 0:N], ACT.Exp, scale=0.5 / SC_K ** 2,
                                             bias=nmx[:, 1, i:i + 1], accum_out=zz[:, 1, i:i + 1]))
                    settle()
                    nc.scalar.sem_inc(exp_ready, 1)
                elif o[0] == "guess":
                    s, g = o[1:]
                    k = len(GROUPS[g])
                    n = s * len(GROUPS) + g
                    act.wait_ge(guess_input, n + 1)
                    nc.scalar.activation(tg[:, 0, 0:k], sm[:, 0, 0:k], ACT.Exp).then_inc(guess, 1)
                elif o[0] in ("into", "carry"):
                    n = BANK[o]
                    if o == ("into", 0):
                        act.wait_ge(h_lo, NT)
                    act.wait_ge(bank_full, n + 1)
                    hi_and_copy(o, bank[n % BANKS][:, :], 1.0 / SC_U, rhs16[:, o[1], 0, :],
                                copy32[:, COPIES[o] % RING, :], bank_read_scalar)
                elif o[0] == "first":
                    n = BANK[o]
                    if o[1] == 0:
                        act.wait_ge(adj_lo, NT)
                    act.wait_ge(bank_full, n + 1)
                    did(nc.scalar.activation(mix[:, o[1], :], bank[n % BANKS][:, :], ACT.Copy, scale=1.0 / SC_U))
                    settle()
                    nc.scalar.sem_inc(bank_read_scalar, 1)
                elif o[0] == "rowsum":
                    n = BANK[o]
                    r_ = rows(NT - 1)
                    act.wait_ge(rowsum_ones, 1)
                    act.wait_ge(bank_full, n + 1)
                    did(nc.scalar.activation(rinv[:, 0:NT - 1], bank[n % BANKS][:, 0:NT - 1], ACT.Copy,
                                             scale=1.0 / SC_S))
                    did(nc.scalar.activation(rinv[0:r_, NT - 1:NT], bank[n % BANKS][0:r_, NT - 1:NT], ACT.Copy,
                                             scale=1.0 / SC_S))
                    settle()
                    nc.scalar.sem_inc(bank_read_scalar, 1)
                    nc.scalar.sem_inc(rowsum_ready, 1)
                elif o[0] == "base":
                    n = BANK[o]
                    act.wait_ge(bank_full, n + 1)
                    copy_only(o, bank[n % BANKS][:, :], 1.0 / SC_U, bank_read_scalar)
                elif o[0] == "spread":
                    s, t = o[1:]
                    n = BANK[o]
                    if s == 0 and t == 0:
                        act.wait_ge(rowsum_inverted, 1)
                    act.wait_ge(bank_full, n + 1)
                    copy_only(o, bank[n % BANKS][:, :], rinv[:, t:t + 1], bank_read_scalar)
                    if s == 0:
                        m = COPIES[o + ("sum",)]
                        act.wait_ge(split, m)
                        did(nc.scalar.activation(mix16[:, t, 0, :], copy32[:, m % RING, :], ACT.Copy))
                        settle()
                        nc.scalar.sem_inc(copied, 1)
                elif o[0] == "cut":
                    s, t = o[1:]
                    r = CUTS[o[1:]] % 2
                    if s == 0 and t == 0:
                        act.wait_ge(bank_full, BANK[("into", NT - 1)] + 1)
                    if CUTS[o[1:]] >= 2:
                        k = CUTS[o[1:]] - 2
                        prev = ("attend", k // NT, k % NT)
                        act.wait_ge(bank_full, BANK[prev] + 1)
                    for b, blocks in enumerate(BLOCKS):
                        n = TURN[o + (b,)]
                        a, e = blocks[0] * P, (blocks[-1] + 1) * P
                        act.wait_ge(turn_full, n + 1)
                        hi_and_copy(o + (b,), turn[n % TURNS][:, 0:e - a], SC_P, attT[:, r, 0, a:e],
                                    copy32[:, COPIES[o + (b,)] % RING, 0:e - a], turn_read_scalar)
                elif o[:2] == ("attend", 1):
                    act.wait_ge(bank_full, BANK[o] + 1)
                    copy_only(o, bank[BANK[o] % BANKS][:, :], rzs[:, o[2]:o[2] + 1], bank_read_scalar)
                elif o[0] == "attend":
                    s, t = o[1:]
                    n = BANK[o]
                    act.wait_ge(bank_full, n + 1)
                    if t > 0:
                        act.wait_ge(turn_full, TURN[("turn", t - 1)] + 1)
                    did(nc.scalar.activation(xnat[:, :], bank[n % BANKS][:, :], ACT.Copy, scale=rzs[:, t:t + 1]))
                    settle()
                    nc.scalar.sem_inc(xa_ready, 1)
                    nc.scalar.sem_inc(bank_read_scalar, 1)
                elif o[0] == "turn":
                    t = o[1]
                    n = TURN[o]
                    act.wait_ge(turn_full, n + 1)
                    src = turn[n % TURNS][:, :].rearrange("p (c n) -> p c n", c=DC)[:, :, 0:rows(t)]
                    cp = copy32[:, COPIES[o] % RING, :].rearrange("p (c n) -> p c n", c=DC)[:, :, 0:rows(t)]
                    hi_and_copy(o, src, SC_X, xT[:, :, 0, t * P:t * P + rows(t)], cp, turn_read_scalar)

        @block.vector
        def _(v):
            steps = [0]

            def did(ins):
                steps[0] += 1
                return ins.then_inc(vector_steps, 1)

            def settle():
                v.wait_ge(vector_steps, steps[0])

            def step(ins):
                did(ins)
                settle()

            def rsqrt(y, r, w):
                step(nc.vector.tensor_scalar(r.bitcast(INT32), y.bitcast(INT32), -0.5, RSQRT_BITS, ALU.mult, ALU.add))
                for _ in range(3):
                    step(nc.vector.tensor_tensor(w, r, r, ALU.mult))
                    step(nc.vector.tensor_tensor(w, w, y, ALU.mult))
                    step(nc.vector.tensor_scalar(w, w, -0.5, 1.5, ALU.mult, ALU.add))
                    step(nc.vector.tensor_tensor(r, r, w, ALU.mult))

            halves = [work[:, :].bitcast(FP16)[:, h * N:(h + 1) * N] for h in range(2)]

            def mass(p, i, cut, dst, scratch=work[:, :]):
                return nc.vector.scalar_tensor_tensor(out=scratch, in0=p[:, i, :], scalar=cut, in1=p[:, i, :],
                                                      op0=ALU.is_ge, op1=ALU.mult, accum_out=dst)

            def below(p, i, bound, dst=None):
                return nc.vector.scalar_tensor_tensor(out=work[:, :], in0=p[:, i, :], scalar=bound, in1=p[:, i, :],
                                                      op0=ALU.is_lt, op1=ALU.mult, accum_out=dst)

            def window(p, i, fence):
                fence(below(p, i, high[:, 0, i:i + 1]))
                fence(nc.vector.max(top8[:, i, :], work[:, :]))
                fence(mass(p, i, top8[:, i, 7:8], tg[:, 1, i:i + 1]))

            def upper_bound_moves(k, fence):
                K = slice(0, k)
                fence(nc.vector.tensor_tensor(msk[:, 0, K], tg[:, 1, K], tgt[:, K], ALU.is_lt))
                fence(nc.vector.tensor_copy(tg[:, 0, K], top8[:, K, 7]))
                fence(nc.vector.copy_predicated(high[:, :, K], msk[:, 0:1, K].broadcast_to((P, 2, k)), tg[:, :, K]))

            def cuts(k, go, fence):
                K = slice(0, k)
                for i in range(k):
                    go(nc.vector.tensor_tensor_scan(pre8[:, i, :], top8[:, i, :], top8[:, i, :],
                                                    high[:, 1, i:i + 1], ALU.add, ALU.max))
                fence(nc.vector.tensor_tensor(sm[:, 5, K], tg[:, 1, K], tgt[:, K], ALU.is_lt))
                tgt8 = tgt[:, K].rearrange("p (k a) -> p k a", a=1).broadcast_to((P, k, 8))
                go(nc.vector.tensor_tensor(sm[:, 4, K], tg[:, 1, K], pre8[:, K, 7], ALU.subtract))
                fence(nc.vector.tensor_tensor(wk8[:, K, :], pre8[:, K, :], tgt8, ALU.is_ge))
                fence(nc.vector.tensor_tensor(wk8[:, K, :], wk8[:, K, :], top8[:, K, :], ALU.mult))
                fence(nc.vector.tensor_reduce(vcut[:, K], wk8[:, K, :], AX.X, ALU.max))
                fence(nc.vector.tensor_tensor(vcut[:, K], vcut[:, K], top8[:, K, 7], ALU.max))
                v8 = vcut[:, K].rearrange("p (k a) -> p k a", a=1).broadcast_to((P, k, 8))
                go(nc.vector.reciprocal(sm[:, 2, K], vcut[:, K]))
                go(nc.vector.tensor_tensor(wk8[:, K, :], top8[:, K, :], v8, ALU.is_gt))
                fence(nc.vector.tensor_tensor(eq8[:, K, :], top8[:, K, :], v8, ALU.is_equal))
                go(nc.vector.tensor_tensor(wk8[:, K, :], wk8[:, K, :], top8[:, K, :], ALU.mult))
                go(nc.vector.tensor_reduce(sm[:, 3, K], eq8[:, K, :], AX.X, ALU.add))
                fence(nc.vector.tensor_tensor(sm[:, 4, K], sm[:, 4, K], sm[:, 2, K], ALU.mult))
                go(nc.vector.tensor_reduce(sm[:, 0, K], wk8[:, K, :], AX.X, ALU.add))
                fence(nc.vector.tensor_tensor(sm[:, 4, K], sm[:, 4, K], eq8[:, K, 7], ALU.mult))
                go(nc.vector.tensor_tensor(sm[:, 3, K], sm[:, 3, K], sm[:, 4, K], ALU.add))
                fence(nc.vector.tensor_tensor(sm[:, 0, K], sm[:, 0, K], high[:, 1, K], ALU.add))
                go(nc.vector.tensor_scalar(sm[:, 3, K], sm[:, 3, K], ROUND_INT, -ROUND_INT, ALU.add, ALU.add))
                fence(nc.vector.tensor_tensor(sm[:, 1, K], tgt[:, K], sm[:, 0, K], ALU.subtract))
                fence(nc.vector.tensor_tensor(sm[:, 1, K], sm[:, 1, K], sm[:, 2, K], ALU.mult))
                fence(nc.vector.tensor_scalar(q1[:, K], sm[:, 1, K], 0.5, 1.0, ALU.max, ALU.add))
                fence(nc.vector.tensor_tensor(sm[:, 3, K], sm[:, 3, K], q1[:, K], ALU.is_ge))
                fence(nc.vector.scalar_tensor_tensor(out=sm[:, 3, K], in0=sm[:, 5, K], scalar=OPEN, in1=sm[:, 3, K],
                                                     op0=ALU.mult, op1=ALU.add))
                fence(nc.vector.tensor_reduce(flag[:, 0:1], sm[:, 3, K], AX.X, ALU.max))
                fence(nc.vector.transpose(flagT[:, :], flag[:, :]))
                fence(nc.vector.tensor_reduce(anyf[:, 0:1], flagT[:, :], AX.X, ALU.max))
                for q in range(4):
                    (fence if q == 3 else go)(nc.vector.tensor_copy(any4[0:1, q:q + 1], anyf[32 * q:32 * q + 1, 0:1]))
                fence(nc.vector.tensor_reduce(anyi[0:1, 0:1], any4[0:1, :], AX.X, ALU.max))

            nc.vector.memset(rhs[64:P, NT - 1, :], 0.0).then_inc(x_padded, 1)
            v.wait_ge(x_padded, 1)
            for half, tiles in enumerate(LN_HALVES):
                a, e = tiles[0], tiles[-1] + 1
                v.wait_ge(x_loaded[half], 16 * (1 + half))
                for t in tiles:
                    did(nc.vector.bn_stats(bst[:, t, :], rhs[:, t, :]))
                settle()
                for t in tiles:
                    did(nc.vector.bn_aggr(mv[:, t, :], bst[:, t, :]))
                settle()
                step(nc.vector.tensor_scalar(lnw[:, 0, a:e], mv[:, a:e, 1], LN_EPS, None, ALU.add))
                rsqrt(lnw[:, 0, a:e], lnw[:, 2, a:e], lnw[:, 3, a:e])
                step(nc.vector.scalar_tensor_tensor(out=lnw[:, 4, a:e], in0=mv[:, a:e, 0], scalar=-1.0,
                                                    in1=lnw[:, 2, a:e], op0=ALU.mult, op1=ALU.mult))
                nc.vector.sem_inc(stats, 1)
            v.wait_ge(w_loaded, 48)
            v.wait_ge(w_hi, 1)
            nc.vector.scalar_tensor_tensor(out=w16[:, :, 1, :], in0=wst[:, :, :], scalar=SC_U, in1=w16[:, :, 0, :],
                                           op0=ALU.mult, op1=ALU.subtract).then_inc(w_lo, 1)
            nc.vector.memset(rinv[:, :], 1.0).then_inc(rowsum_ones, 1)
            step(nc.vector.memset(flag[:, :], 0.0))
            step(nc.vector.memset(anyf[:, :], 0.0))
            for t in range(NT):
                v.wait_ge(h_hi, t + 1)
                nc.vector.scalar_tensor_tensor(out=feat16[:, t, 1, :], in0=rhs[:, t, :], scalar=SC_X,
                                               in1=feat16[:, t, 0, :], op0=ALU.mult, op1=ALU.subtract).then_inc(h_lo, 1)
                n = TURN[("ht", t)]
                v.wait_ge(turn_read_scalar, n + 1)
                nc.vector.scalar_tensor_tensor(out=xT[:, :, 1, t * P:t * P + rows(t)],
                                               in0=turn[n % TURNS][:, :].rearrange("p (c n) -> p c n", c=DC)[:, :, 0:rows(t)],
                                               scalar=SC_X, in1=xT[:, :, 0, t * P:t * P + rows(t)],
                                               op0=ALU.mult, op1=ALU.subtract).then_inc(turn_read_vector, 1)
            for o in ORDER:
                if o[0] == "qk":
                    s, c = o[1:]
                    n = BANK[o]
                    a, w = CHUNKS[c]
                    v.wait_ge(k_hi, s * len(CHUNKS) + c + 1)
                    nc.vector.scalar_tensor_tensor(out=kq16[:, 1, a:a + w], in0=bank[n % BANKS][0:DA, 0:w],
                                                   scalar=SC_K / (SC_X * SC_U), in1=kq16[:, 0, a:a + w],
                                                   op0=ALU.mult, op1=ALU.subtract).then_inc(bank_read_vector, 1)
                elif o[0] == "q2":
                    s, c = o[1:]
                    n = TURN[o]
                    a, w = CHUNKS[c]
                    v.wait_ge(turn_read_scalar, n + 1)
                    lo = nc.vector.scalar_tensor_tensor(out=kq16[:, 3, a:a + w], in0=turn[n % TURNS][0:DA, 0:w],
                                                        scalar=SC_K, in1=kq16[:, 2, a:a + w],
                                                        op0=ALU.mult, op1=ALU.subtract)
                    if c == len(CHUNKS) - 1:
                        step(lo)
                        pad = NT * P - N
                        lo = nc.vector.tensor_copy(kq16[:, 2:4, N:N + pad], kq16[:, 2:4, N - pad:N])
                    lo.then_inc(turn_read_vector, 1)
                elif o[0] == "invert":
                    v.wait_ge(rowsum_ready, 1)
                    step(nc.vector.tensor_scalar(rinv[:, :], rinv[:, :], 1e-12, None, ALU.max))
                    step(nc.vector.reciprocal(rinv[:, :], rinv[:, :]))
                    step(nc.vector.tensor_scalar(rinv[:, :], rinv[:, :], 1.0 / SC_S, None, ALU.mult))
                    nc.vector.sem_inc(rowsum_inverted, 1)
                elif o[0] == "logits":
                    s, t = o[1:]
                    i = place(s, t)[2]
                    n = LOGITS[o[1:]]
                    lg = lgs[logits_bank(s, t)]
                    v.wait_ge(logits_ready, n + 1)
                    step(nc.vector.reduce_max(mx[:, i:i + 1], lg[:, 0:N], AX.X))
                    did(nc.vector.tensor_scalar(nmx[:, 0, i:i + 1], mx[:, i:i + 1], -1.0 / SC_K ** 2, None, ALU.mult))
                    did(nc.vector.tensor_scalar(nmx[:, 1, i:i + 1], mx[:, i:i + 1], -0.5 / SC_K ** 2, None, ALU.mult))
                    settle()
                    nc.vector.sem_inc(max_ready, 1)
                elif o[0] == "guess":
                    s, g = o[1:]
                    group = GROUPS[g]
                    k = len(group)
                    K = slice(0, k)
                    Z = slice((g % 2) * SLOTS, (g % 2) * SLOTS + k)
                    ng = s * len(GROUPS) + g
                    v.wait_ge(exp_ready, s * NT + group[-1] + 1)
                    step(nc.vector.tensor_scalar(sm[:, 1, K], zbits[:, 0, Z], GUESS[0] * LOG_BITS,
                                                 GUESS[2] - (GUESS[0] + GUESS[1]) * LOG_ONE, ALU.mult, ALU.add))
                    step(nc.vector.scalar_tensor_tensor(out=sm[:, 0, K], in0=zbits[:, 1, Z], scalar=GUESS[1] * LOG_BITS,
                                                        in1=sm[:, 1, K],
                                                        op0=ALU.mult, op1=ALU.add))
                    nc.vector.sem_inc(guess_input, 1)
                    did(nc.vector.tensor_scalar(tgt[:, K], zz[:, 0, Z], P_TOP, None, ALU.mult))
                    did(nc.vector.memset(high[:, 0, K], HI0))
                    did(nc.vector.memset(high[:, 1, K], 0.0))
                    did(nc.vector.memset(low[:, 0, K], 0.0))
                    did(nc.vector.tensor_copy(low[:, 1, K], zz[:, 0, Z]))
                    v.wait_ge(guess, ng + 1)
                    step(nc.vector.tensor_scalar(tg[:, 0, K], tg[:, 0, K], 1.0, None, ALU.min))
                elif o[0] == "round":
                    s, g, e = o[1:]
                    k = len(GROUPS[g])
                    K = slice(0, k)
                    p = probs[place(s, GROUPS[g][0])[0]]
                    for i in range(k):
                        if i >= 2:
                            v.wait_ge(vector_steps, steps[0] - 1)
                        did(mass(p, i, tg[:, 0, i:i + 1], tg[:, 1, i:i + 1], halves[i % 2]))
                    settle()
                    did(nc.vector.tensor_tensor(msk[:, 0, K], tg[:, 1, K], tgt[:, K], ALU.is_ge))
                    step(nc.vector.tensor_tensor(msk[:, 1, K], tg[:, 1, K], tgt[:, K], ALU.is_lt))
                    did(nc.vector.copy_predicated(low[:, :, K], msk[:, 0:1, K].broadcast_to((P, 2, k)), tg[:, :, K]))
                    step(nc.vector.copy_predicated(high[:, :, K], msk[:, 1:2, K].broadcast_to((P, 2, k)), tg[:, :, K]))
                    if e == EVALS[s] - 1:
                        continue
                    did(nc.vector.tensor_tensor(dif[:, :, K], high[:, :, K], low[:, :, K], ALU.subtract))
                    step(nc.vector.tensor_tensor(sm[:, 1, K], low[:, 1, K], tgt[:, K], ALU.subtract))
                    did(nc.vector.reciprocal(sm[:, 0, K], dif[:, 1, K]))
                    step(nc.vector.scalar_tensor_tensor(out=sm[:, 1, K], in0=low[:, 0, K], scalar=4.0, in1=sm[:, 1, K],
                                                        op0=ALU.mult, op1=ALU.add))
                    step(nc.vector.scalar_tensor_tensor(out=sm[:, 1, K], in0=sm[:, 1, K], scalar=-1.0, in1=sm[:, 0, K],
                                                        op0=ALU.mult, op1=ALU.mult))
                    step(nc.vector.tensor_scalar(sm[:, 1, K], sm[:, 1, K], 0.02, 0.98, ALU.max, ALU.min))
                    step(nc.vector.tensor_tensor(sm[:, 1, K], sm[:, 1, K], dif[:, 0, K], ALU.mult))
                    step(nc.vector.tensor_tensor(tg[:, 0, K], sm[:, 1, K], low[:, 0, K], ALU.add))
                elif o[0] == "window":
                    s, g, w = o[1:]
                    k = len(GROUPS[g])
                    p = probs[place(s, GROUPS[g][0])[0]]
                    K = slice(0, k)
                    Z = slice((g % 2) * SLOTS, (g % 2) * SLOTS + k)
                    if w == 0:
                        for i in range(k):
                            step(below(p, i, high[:, 0, i:i + 1]))
                            step(nc.vector.max(top8[:, i, :], work[:, :]))
                    else:
                        for i in range(k):
                            step(below(p, i, top8[:, i, 7:8], sm[:, 6, i:i + 1]))
                            step(nc.vector.max(next8[:, i, :], work[:, :]))
                        did(nc.vector.tensor_copy(tg[:, 0, K], top8[:, K, 7]))
                        step(nc.vector.tensor_tensor(tg[:, 1, K], zz[:, 0, Z], sm[:, 6, K], ALU.subtract))
                        step(nc.vector.tensor_tensor(msk[:, 0, K], tg[:, 1, K], tgt[:, K], ALU.is_lt))
                        did(nc.vector.copy_predicated(high[:, :, K], msk[:, 0:1, K].broadcast_to((P, 2, k)), tg[:, :, K]))
                        step(nc.vector.copy_predicated(top8[:, K, :], msk[:, 0, K].rearrange("p (k a) -> p k a", a=1)
                                                       .broadcast_to((P, k, 8)), next8[:, K, :]))
                    if w == WINDOWS[s] - 1:
                        for i in range(k):
                            if i >= 2:
                                v.wait_ge(vector_steps, steps[0] - 1)
                            did(mass(p, i, top8[:, i, 7:8], tg[:, 1, i:i + 1], halves[i % 2]))
                        settle()
                elif o[0] == "found":
                    s, g = o[1:]
                    k = len(GROUPS[g])
                    p = probs[place(s, GROUPS[g][0])[0]]
                    cuts(k, did, step)

                    def some_row_is_open():
                        worst[0] = v.value_load(anyi[0:1, 0:1], min_val=0, max_val=int(OPEN) + 1)
                        return worst[0] >= int(OPEN)

                    def fence(ins):
                        nc.vector.drain()

                    with v.While(some_row_is_open):
                        upper_bound_moves(k, fence)
                        for i in range(k):
                            window(p, i, fence)
                        cuts(k, fence, fence)
                elif o[0] == "cut":
                    s, t = o[1:]
                    b, i = place(s, t)[:2]
                    p = probs[b]
                    tie = worst[0]
                    with v.If(tie < 1):
                        nc.vector.scalar_tensor_tensor(out=p[:, i, :], in0=p[:, i, :], scalar=vcut[:, i:i + 1],
                                                       in1=p[:, i, :], op0=ALU.is_ge, op1=ALU.mult,
                                                       accum_out=zk[:, i:i + 1])
                        nc.vector.drain()
                    with v.If(tie > 0):
                        nc.vector.tensor_scalar(side, p[:, i, :], vcut[:, i:i + 1], 2.0 ** 60,
                                                ALU.subtract, ALU.mult)
                        nc.vector.drain()
                        nc.vector.tensor_scalar(rk16, side, 0.0, None, ALU.is_equal)
                        nc.vector.drain()
                        nc.vector.tensor_tensor_scan(rk16, rk16, rk16, 0.0, ALU.add, ALU.max)
                        nc.vector.drain()
                        nc.vector.scalar_tensor_tensor(out=side, in0=rk16, scalar=q1[:, i:i + 1], in1=side,
                                                       op0=ALU.is_lt, op1=ALU.add)
                        nc.vector.drain()
                        nc.vector.scalar_tensor_tensor(out=p[:, i, :], in0=side, scalar=0.5, in1=p[:, i, :],
                                                       op0=ALU.is_gt, op1=ALU.mult, accum_out=zk[:, i:i + 1])
                        nc.vector.drain()
                    did(nc.vector.reciprocal(rzs[:, t:t + 1], zk[:, i:i + 1]))
                    settle()
                    step(nc.vector.tensor_scalar(rzs[:, t:t + 1], rzs[:, t:t + 1],
                                                 1.0 / (SC_P * SC_X) if s == 0 else 1.0 / SC_P, None, ALU.mult))
                    nc.vector.sem_inc(kept_ready, 1)
                elif o[0] == "norm":
                    tiles = NORMS[o[1]]
                    a, e = tiles[0], tiles[-1] + 1
                    v.wait_ge(split, max(COPIES[kind, 1, t] for kind in ("spread", "attend") for t in tiles) + 1)
                    for t in tiles:
                        did(nc.vector.bn_stats(bst[:, t, :], feat[:, t, :]))
                    settle()
                    for t in tiles:
                        did(nc.vector.bn_aggr(mv[:, t, :], bst[:, t, :]))
                    settle()
                    step(nc.vector.tensor_scalar(lnw[:, 0, a:e], mv[:, a:e, 1], LN_EPS * SC_X ** 2, None, ALU.add))
                    rsqrt(lnw[:, 0, a:e], lnw[:, 2, a:e], lnw[:, 3, a:e])
                    v.wait_ge(gamma_beta_loaded, 32)
                    for t in tiles:
                        r_ = rows(t)
                        did(nc.vector.scalar_tensor_tensor(out=feat[0:r_, t, :], in0=feat[0:r_, t, :],
                                                           scalar=mv[0:r_, t, 0:1], in1=ust[0:r_, 2, :],
                                                           op0=ALU.subtract, op1=ALU.mult))
                    for k, t in enumerate(tiles):
                        r_ = rows(t)
                        v.wait_ge(vector_steps, steps[0] - (len(tiles) - 1 - k))
                        v.wait_ge(residual_ready, t + 1)
                        nc.vector.scalar_tensor_tensor(out=feat[0:r_, t, :], in0=feat[0:r_, t, :],
                                                       scalar=lnw[0:r_, 2, t:t + 1], in1=mix[0:r_, t, :],
                                                       op0=ALU.mult, op1=ALU.add).then_inc(out_ready, 1)

        @block.tensor
        def _(pe):
            def three(dst, l_hi, l_lo, r_hi, r_lo, first, last):
                nc.tensor.matmul(dst, l_hi, r_hi, start=first, stop=False)
                nc.tensor.matmul(dst, l_hi, r_lo, start=False, stop=False)
                return nc.tensor.matmul(dst, l_lo, r_hi, start=False, stop=last)

            def free(jobs_by, n, ring, sem_a, sem_v):
                if n >= ring:
                    for who, read in (("a", sem_a), ("v", sem_v)):
                        if who in jobs_by[n - ring]:
                            pe.wait_ge(read, reads(jobs_by, n - ring, who))

            pe.wait_ge(constants_ready, 2)
            for t in range(NT):
                n = TURN[("ht", t)]
                pe.wait_ge(h_ready, t + 1)
                free(TURN_BY, n, TURNS, turn_read_scalar, turn_read_vector)
                r_ = rows(t)
                for c in range(DC):
                    last = nc.tensor.transpose(turn[n % TURNS][:, c * P:c * P + r_], rhs[0:r_, t, c * P:(c + 1) * P],
                                               ident[0:r_, 0:r_])
                last.then_inc(turn_full, 1)

            for o in ORDER:
                if o[0] == "qk":
                    s, c = o[1:]
                    n = BANK[o]
                    a, w = CHUNKS[c]
                    if s == 0 and c == 0:
                        pe.wait_ge(w_lo, 1)
                        pe.wait_ge(turn_read_vector, NT)
                    if s == 1:
                        pe.wait_ge(split, COPIES[("turn", (a + w - 1) // P)] + 1)
                    free(BANK_BY, n, BANKS, bank_read_scalar, bank_read_vector)
                    for d in range(DC):
                        last = three(bank[n % BANKS][:, 0:w], w16[:, d, 0, :], w16[:, d, 1, :],
                                     xT[:, d, 0, a:a + w], xT[:, d, 1, a:a + w], d == 0, d == DC - 1)
                    last.then_inc(bank_full, 1)
                elif o[0] == "q2":
                    s, c = o[1:]
                    n = TURN[o]
                    a, w = CHUNKS[c]
                    pe.wait_ge(q_ready, s * len(CHUNKS) + c + 1)
                    free(TURN_BY, n, TURNS, turn_read_scalar, turn_read_vector)
                    nc.tensor.matmul(turn[n % TURNS][0:DA, 0:w], w2sb[DA:P, :], work[DA:P, a:a + w],
                                     start=True, stop=True).then_inc(turn_full, 1)
                elif o[0] == "logits":
                    s, t = o[1:]
                    n = LOGITS[o[1:]]
                    if t == 0:
                        pe.wait_ge(bank_read_vector, reads(BANK_BY, BANK[("qk", s, len(CHUNKS) - 1)], "v"))
                        pe.wait_ge(turn_read_vector, reads(TURN_BY, TURN[("q2", s, len(CHUNKS) - 1)], "v"))
                    lg = lgs[logits_bank(s, t)]
                    if t == 1:
                        last = TURN[("q2", s, len(CHUNKS) - 1)]
                        pe.wait_ge(turn_read_scalar, reads(TURN_BY, last, "a"))
                        pe.wait_ge(turn_read_vector, reads(TURN_BY, last, "v"))
                    elif t in (2, 3) or (s == 1 and t in GROUPS[1]):
                        pe.wait_ge(exp_ready, n - 1)
                    elif n:
                        pe.wait_ge(exp_ready, n)
                    for j, (a, w) in enumerate(CHUNKS):
                        last = three(lg[:, a:a + w], kq16[:, 2, t * P:(t + 1) * P], kq16[:, 3, t * P:(t + 1) * P],
                                     kq16[:, 0, a:a + w], kq16[:, 1, a:a + w], True, True)
                    last.then_inc(logits_ready, 1)
                elif o[0] in ("into", "first", "carry", "base"):
                    t = o[1]
                    n = BANK[o]
                    if t == 0:
                        pe.wait_ge(u_lo, {"into": 1, "first": 2, "carry": 3, "base": 4}[o[0]])
                    u16 = {"into": ub16, "first": ua16, "carry": ua16, "base": ub16}[o[0]]
                    free(BANK_BY, n, BANKS, bank_read_scalar, bank_read_vector)
                    r_ = rows(t)
                    for d in range(DC):
                        last = three(bank[n % BANKS][0:r_, :], xT[:, d, 0, t * P:t * P + r_], xT[:, d, 1, t * P:t * P + r_],
                                     u16[:, d, 0, :], u16[:, d, 1, :], d == 0, d == DC - 1)
                    last.then_inc(bank_full, 1)
                elif o[0] == "rowsum":
                    n = BANK[o]
                    pe.wait_ge(adj_lo, NT)
                    free(BANK_BY, n, BANKS, bank_read_scalar, bank_read_vector)
                    for t in range(NT):
                        for kt in range(NT):
                            for half in range(2):
                                last = nc.tensor.matmul(bank[n % BANKS][0:rows(t), t:t + 1],
                                                        adj16[0:rows(kt), half, kt, t * P:t * P + rows(t)],
                                                        ones16[0:rows(kt), 0:1], start=(kt + half == 0),
                                                        stop=(kt == NT - 1 and half == 1))
                    last.then_inc(bank_full, 1)
                elif o[0] == "spread":
                    s, t = o[1:]
                    n = BANK[o]
                    if t == 0:
                        if s == 0:
                            pe.wait_ge(split, COPIES[("into", NT - 1)] + 1)
                        else:
                            pe.wait_ge(split, COPIES[("spread", 0, NT - 1, "sum")] + 1)
                    free(BANK_BY, n, BANKS, bank_read_scalar, bank_read_vector)
                    src = rhs16 if s == 0 else mix16
                    r_ = rows(t)
                    for kt in range(NT):
                        k_ = rows(kt)
                        last = three(bank[n % BANKS][0:r_, :], adj16[0:k_, 0, kt, t * P:t * P + r_],
                                     adj16[0:k_, 1, kt, t * P:t * P + r_], src[0:k_, kt, 0, :], src[0:k_, kt, 1, :],
                                     kt == 0, kt == NT - 1)
                    last.then_inc(bank_full, 1)
                elif o[0] == "cut":
                    s, t = o[1:]
                    b, i = place(s, t)[:2]
                    p = probs[b]
                    pe.wait_ge(kept_ready, CUTS[o[1:]] + 1)
                    r_ = rows(t)
                    for h, blocks in enumerate(BLOCKS):
                        n = TURN[o + (h,)]
                        free(TURN_BY, n, TURNS, turn_read_scalar, turn_read_vector)
                        for j, kt in enumerate(blocks):
                            last = nc.tensor.transpose(turn[n % TURNS][0:rows(kt), j * P:j * P + r_],
                                                       p[0:r_, i, kt * P:kt * P + rows(kt)], ident[0:r_, 0:r_])
                        last.then_inc(turn_full, 1)
                elif o[0] == "attend":
                    s, t = o[1:]
                    n = BANK[o]
                    r = ATTENDS[o[1:]] % 2
                    pe.wait_ge(split, COPIES[("cut", s, t, len(BLOCKS) - 1)] + 1)
                    if t == 0:
                        if s == 0:
                            pe.wait_ge(h_lo, NT)
                        else:
                            pe.wait_ge(split, COPIES[("carry", NT - 1)] + 1)
                    free(BANK_BY, n, BANKS, bank_read_scalar, bank_read_vector)
                    src = feat16 if s == 0 else rhs16
                    r_ = rows(t)
                    for kt in range(NT):
                        k_ = rows(kt)
                        last = three(bank[n % BANKS][0:r_, :], attT[0:k_, r, 0, kt * P:kt * P + r_],
                                     attT[0:k_, r, 1, kt * P:kt * P + r_], src[0:k_, kt, 0, :], src[0:k_, kt, 1, :],
                                     kt == 0, kt == NT - 1)
                    last.then_inc(bank_full, 1)
                elif o[0] == "turn":
                    t = o[1]
                    n = TURN[o]
                    pe.wait_ge(xa_ready, t + 1)
                    free(TURN_BY, n, TURNS, turn_read_scalar, turn_read_vector)
                    r_ = rows(t)
                    for c in range(DC):
                        last = nc.tensor.transpose(turn[n % TURNS][:, c * P:c * P + r_], xnat[0:r_, c * P:(c + 1) * P],
                                                   ident[0:r_, 0:r_])
                    last.then_inc(turn_full, 1)


def kernel(**inputs):
    import numpy as np
    import concourse.bacc as bacc
    from concourse.bass_utils import run_bass_kernel_spmd as run

    nc = bacc.Bacc("TRN2", target_bir_lowering=False, num_devices=1, dynamic_dma_scratch_size=1024)
    names = ["x", "adj_t", "w1", "w2", "w3", "u10", "u11", "u20", "u21", "gamma", "beta"]
    src = {"x": "x", "w1": "L0_gnn_W1", "w2": "L0_gnn_W2", "w3": "L0_gnn_W3", "u10": "L0_gnn_U1_0",
           "u11": "L0_gnn_U1_1", "u20": "L0_gnn_U2_0", "u21": "L0_gnn_U2_1", "gamma": "L0_gnn_gamma",
           "beta": "L0_gnn_beta"}
    arrays, args = {}, []
    for n in names:
        a = np.ascontiguousarray(np.asarray(inputs["adj"]).T if n == "adj_t" else inputs[src[n]])
        arrays[n] = a
        args.append(nc.dram_tensor(n, a.shape, mybir.dt.from_np(a.dtype), kind="ExternalInput").ap())
    o = nc.dram_tensor("out", (N, D), FP32, kind="ExternalOutput").ap()
    graph_kernel(nc, *args, o)
    return run(nc, [arrays], core_ids=[0]).results[0]["out"]
```
